# Optimizing a Trainium2 kernel written in Bass

```python
import numpy as np
import jax
import jax.numpy as jnp

def _softmax(x, axis=-1):
    return jax.nn.softmax(x, axis=axis)

def _gelu(x):
    return jax.nn.gelu(x, approximate=True)

def _silu(x):
    return jax.nn.silu(x)

def _sigmoid(x):
    return jax.nn.sigmoid(x)

def _layernorm(x, axis=-1, eps=1e-05):
    m = jnp.mean(x, axis=axis, keepdims=True)
    v = jnp.var(x, axis=axis, keepdims=True)
    return (x - m) / jnp.sqrt(v + eps)

def _scatter_add(tgt, idx, src, axis=0):
    return tgt.at[idx].add(src)

def _segment_sum(src, seg, n):
    return jax.ops.segment_sum(src, seg, n)
kernel_name = 'mk_adaln_attn_ffn_d1_seqx_r8_2be867'

def setup_inputs(seed: int=0):
    np.random.seed(seed)
    _w = jnp.asarray

    def _rec_inputs():
        import jax
        import jax.numpy as jnp
        _rk = jax.random.key(seed)
        x = -0.000125 + 0.9999 * jax.random.normal(jax.random.fold_in(_rk, 1), (128, 32, 256), jnp.float32)
        _lenS = 32 - jax.random.randint(jax.random.fold_in(_rk, 7), (128,), 0, max(1, 32 // 4) + 1, jnp.int32)
        _lenS2 = 32 - jax.random.randint(jax.random.fold_in(_rk, 8), (128,), 0, max(1, 32 // 4) + 1, jnp.int32)
        itok_B_0_7 = jax.random.randint(jax.random.fold_in(_rk, 11), (128,), 0, 8, jnp.int32)
        fside_8xS_0 = -0.00162727 + 0.0609077 * jax.random.normal(jax.random.fold_in(_rk, 12), (8, 32), jnp.float32)
        itok_B_0_6 = jax.random.randint(jax.random.fold_in(_rk, 13), (128,), 0, 7, jnp.int32)
        return (x, itok_B_0_7, fside_8xS_0, itok_B_0_6)
    x, itok_B_0_7, fside_8xS_0, itok_B_0_6 = _rec_inputs()

    def _L0_cond_setup():
        import jax, jax.numpy as jnp
        import numpy as np
        B, C, T = (64, 32, 256)
        D, N = (32, 8)
        key = jax.random.key(seed)
        k_x, k_s, k_w, k_b = jax.random.split(key, 4)
        scale = 1.0 / np.sqrt(C)
        x = jax.random.normal(k_x, (B, C, T), dtype=jnp.float32)
        subjects = jax.random.randint(k_s, (B,), 0, N, dtype=jnp.int64)
        weights = jax.random.normal(k_w, (N, C, D), dtype=jnp.float32) * scale
        bias = jax.random.normal(k_b, (N, D), dtype=jnp.float32) * scale
        return {'x': x, 'subjects': subjects, 'weights': weights, 'bias': bias}
    _L0_cond_all = _L0_cond_setup()
    _L0_cond_in = {k: v for k, v in _L0_cond_all.items() if k in ('weights',)}
    del _L0_cond_all

    def _L0_attn_setup():
        import jax, jax.numpy as jnp
        import numpy as np
        import math
        E = 256
        H = 16
        D = E // H

        def _alibi_slopes(n):

            def pow2_slopes(n):
                start = 2 ** (-2 ** (-(math.log2(n) - 3)))
                return [start * start ** i for i in range(n)]
            if math.log2(n).is_integer():
                return pow2_slopes(n)
            c = 2 ** math.floor(math.log2(n))
            return pow2_slopes(c) + _alibi_slopes(2 * c)[::2][:n - c]

        def _alibi_bias(seq_len):
            slopes = jnp.asarray(_alibi_slopes(H), dtype=jnp.float32)
            pos = jnp.arange(seq_len)
            rel = jnp.abs(pos[None, :] - pos[:, None]).astype(jnp.float32)
            return -slopes[:, None, None] * rel[None, :, :]
        key = jax.random.key(seed)
        ks = jax.random.split(key, 5)
        B, S = (2, 256)
        scale = 1.0 / math.sqrt(E)
        x = jax.random.normal(ks[0], (B, S, E), dtype=jnp.float32)
        Wq = jax.random.normal(ks[1], (E, E), dtype=jnp.float32) * scale
        Wk = jax.random.normal(ks[2], (E, E), dtype=jnp.float32) * scale
        Wv = jax.random.normal(ks[3], (E, E), dtype=jnp.float32) * scale
        Wo = jax.random.normal(ks[4], (E, E), dtype=jnp.float32) * scale
        z = jnp.zeros((E,), dtype=jnp.float32)
        return {'x': x, 'Wq': Wq, 'bq': z, 'Wk': Wk, 'bk': z, 'Wv': Wv, 'bv': z, 'Wo': Wo, 'bo': z}
    _L0_attn_all = _L0_attn_setup()
    _L0_attn_in = {k: v for k, v in _L0_attn_all.items() if k in ('Wq', 'bq', 'Wk', 'bk', 'Wv', 'bv', 'Wo', 'bo')}
    del _L0_attn_all

    def _L0_cond2_setup():
        import jax, jax.numpy as jnp
        import numpy as np
        B, T, D_IN, D_OUT = (16, 256, 256, 256)
        N_ADAPTERS, RANK = (8, 16)
        key = jax.random.key(seed)
        k_x, k_w, k_a, k_b, k_s, k_idx = jax.random.split(key, 6)
        x = jax.random.normal(k_x, (B, T, D_IN), dtype=jnp.float32)
        W = jax.random.normal(k_w, (D_OUT, D_IN), dtype=jnp.float32) * (1.0 / np.sqrt(D_IN))
        A = jax.random.normal(k_a, (N_ADAPTERS, RANK, D_IN), dtype=jnp.float32) * 0.02
        Bm = jax.random.normal(k_b, (N_ADAPTERS, D_OUT, RANK), dtype=jnp.float32) * 0.02
        scalings = jnp.ones((N_ADAPTERS,), dtype=jnp.float32)
        adapter_idx = jax.random.randint(k_idx, (B,), 0, N_ADAPTERS, dtype=jnp.int32)
        return {'x': x, 'W': W, 'A': A, 'Bm': Bm, 'scalings': scalings, 'adapter_idx': adapter_idx}
    _L0_cond2_all = _L0_cond2_setup()
    _L0_cond2_in = {k: v for k, v in _L0_cond2_all.items() if k in ('W', 'A', 'Bm', 'scalings')}
    del _L0_cond2_all

    def _L0_ffn_setup():
        import jax, jax.numpy as jnp
        import numpy as np
        H = 256
        F = 128
        E = 32
        G = 8
        TOPK_GROUP = 3
        TOP_K = 6
        N_SHARED = 2
        SCALE = 1.0
        B, S = (1, 256)
        key = jax.random.key(seed)
        ks = jax.random.split(key, 8)
        std = 0.02
        return {'hidden_states': jax.random.normal(ks[0], (B, S, H), dtype=jnp.float32), 'w_gate': jax.random.normal(ks[1], (E, H), dtype=jnp.float32) * std, 'wg': jax.random.normal(ks[2], (E, H, F), dtype=jnp.float32) * std, 'wu': jax.random.normal(ks[3], (E, H, F), dtype=jnp.float32) * std, 'wd': jax.random.normal(ks[4], (E, F, H), dtype=jnp.float32) * std, 'sg': jax.random.normal(ks[5], (N_SHARED * F, H), dtype=jnp.float32) * std, 'su': jax.random.normal(ks[6], (N_SHARED * F, H), dtype=jnp.float32) * std, 'sd': jax.random.normal(ks[7], (H, N_SHARED * F), dtype=jnp.float32) * std}
    _L0_ffn_all = _L0_ffn_setup()
    _L0_ffn_in = {k: v for k, v in _L0_ffn_all.items() if k in ('w_gate', 'wg', 'wu', 'wd', 'sg', 'su', 'sd')}
    del _L0_ffn_all
    return {'x': x, 'itok_B_0_7': itok_B_0_7, 'fside_8xS_0': fside_8xS_0, 'itok_B_0_6': itok_B_0_6, 'L0_cond_weights': _L0_cond_in['weights'], 'L0_attn_Wq': _L0_attn_in['Wq'], 'L0_attn_bq': _L0_attn_in['bq'], 'L0_attn_Wk': _L0_attn_in['Wk'], 'L0_attn_bk': _L0_attn_in['bk'], 'L0_attn_Wv': _L0_attn_in['Wv'], 'L0_attn_bv': _L0_attn_in['bv'], 'L0_attn_Wo': _L0_attn_in['Wo'], 'L0_attn_bo': _L0_attn_in['bo'], 'L0_cond2_W': _L0_cond2_in['W'], 'L0_cond2_A': _L0_cond2_in['A'], 'L0_cond2_Bm': _L0_cond2_in['Bm'], 'L0_cond2_scalings': _L0_cond2_in['scalings'], 'L0_ffn_w_gate': _L0_ffn_in['w_gate'], 'L0_ffn_wg': _L0_ffn_in['wg'], 'L0_ffn_wu': _L0_ffn_in['wu'], 'L0_ffn_wd': _L0_ffn_in['wd'], 'L0_ffn_sg': _L0_ffn_in['sg'], 'L0_ffn_su': _L0_ffn_in['su'], 'L0_ffn_sd': _L0_ffn_in['sd']}

def reference(x, itok_B_0_7, fside_8xS_0, itok_B_0_6, L0_cond_weights, L0_attn_Wq, L0_attn_bq, L0_attn_Wk, L0_attn_bk, L0_attn_Wv, L0_attn_bv, L0_attn_Wo, L0_attn_bo, L0_cond2_W, L0_cond2_A, L0_cond2_Bm, L0_cond2_scalings, L0_ffn_w_gate, L0_ffn_wg, L0_ffn_wu, L0_ffn_wd, L0_ffn_sg, L0_ffn_su, L0_ffn_sd):
    import jax
    import jax.numpy as jnp

    def _L0_cond_ref(x, subjects, weights, bias):
        import jax, jax.numpy as jnp
        import numpy as np
        B, C, T = (64, 32, 256)
        D, N = (32, 8)
        w = weights[subjects]
        b = bias[subjects]
        out = jnp.einsum('bct,bcd->bdt', x, w)
        out = out + b[:, :, None]
        return out

    def _L0_attn_ref(x, Wq, bq, Wk, bk, Wv, bv, Wo, bo):
        import jax, jax.numpy as jnp
        import numpy as np
        import math
        E = 256
        H = 16
        D = E // H

        def _alibi_slopes(n):

            def pow2_slopes(n):
                start = 2 ** (-2 ** (-(math.log2(n) - 3)))
                return [start * start ** i for i in range(n)]
            if math.log2(n).is_integer():
                return pow2_slopes(n)
            c = 2 ** math.floor(math.log2(n))
            return pow2_slopes(c) + _alibi_slopes(2 * c)[::2][:n - c]

        def _alibi_bias(seq_len):
            slopes = jnp.asarray(_alibi_slopes(H), dtype=jnp.float32)
            pos = jnp.arange(seq_len)
            rel = jnp.abs(pos[None, :] - pos[:, None]).astype(jnp.float32)
            return -slopes[:, None, None] * rel[None, :, :]
        B, S, _ = x.shape

        def proj(W, b):
            return (x @ W.T + b).reshape(B, S, H, D).transpose(0, 2, 1, 3)
        q = proj(Wq, bq)
        k = proj(Wk, bk)
        v = proj(Wv, bv)
        scores = jnp.einsum('bhqd,bhkd->bhqk', q, k) / math.sqrt(D)
        causal = jnp.triu(jnp.ones((S, S), dtype=bool), k=1)
        scores = jnp.where(causal[None, None], -jnp.inf, scores)
        scores = scores + _alibi_bias(S)[None]
        probs = jax.nn.softmax(scores, axis=-1)
        out = jnp.einsum('bhqk,bhkd->bhqd', probs, v)
        out = out.transpose(0, 2, 1, 3).reshape(B, S, E)
        return out @ Wo.T + bo

    def _L0_cond2_ref(x, W, A, Bm, scalings, adapter_idx):
        import jax, jax.numpy as jnp
        import numpy as np
        B, T, D_IN, D_OUT = (16, 256, 256, 256)
        N_ADAPTERS, RANK = (8, 16)
        H = jnp.einsum('btd,od->bto', x, W)
        A_b = A[adapter_idx]
        B_b = Bm[adapter_idx]
        s_b = scalings[adapter_idx]
        xa = jnp.einsum('btd,brd->btr', x, A_b)
        delta = jnp.einsum('btr,bor->bto', xa, B_b)
        delta = jax.lax.stop_gradient(delta * s_b[:, None, None])
        return H + delta

    def _L0_ffn_ref(hidden_states, w_gate, wg, wu, wd, sg, su, sd):
        import jax, jax.numpy as jnp
        import numpy as np
        H = 256
        F = 128
        E = 32
        G = 8
        TOPK_GROUP = 3
        TOP_K = 6
        N_SHARED = 2
        SCALE = 1.0
        B, S = (1, 256)
        b, s, h = hidden_states.shape
        x = hidden_states.reshape(-1, h)
        T = x.shape[0]
        logits = x.astype(jnp.float32) @ w_gate.T
        scores = jax.nn.softmax(logits, axis=-1)
        group_scores = scores.reshape(T, G, E // G).max(axis=-1)
        _, group_idx = jax.lax.top_k(group_scores, TOPK_GROUP)
        group_mask = jax.nn.one_hot(group_idx, G, dtype=scores.dtype).sum(axis=1)
        score_mask = jnp.repeat(group_mask, E // G, axis=-1)
        tmp_scores = jnp.where(score_mask > 0.5, scores, 0.0)
        topk_weight, topk_idx = jax.lax.top_k(tmp_scores, TOP_K)
        topk_weight = topk_weight / (topk_weight.sum(axis=-1, keepdims=True) + 1e-20) * SCALE
        combine_w = jnp.zeros((T, E), dtype=jnp.float32)
        combine_w = combine_w.at[jnp.arange(T)[:, None], topk_idx].add(topk_weight)
        g = jnp.einsum('th,ehf->etf', x, wg)
        u = jnp.einsum('th,ehf->etf', x, wu)
        act = jax.nn.silu(g) * u
        act = act * combine_w.T[:, :, None]
        y = jnp.einsum('etf,efh->th', act, wd)
        shared = jax.nn.silu(x @ sg.T) * (x @ su.T) @ sd.T
        return (y + shared).reshape(b, s, h)
    x = x + _L0_attn_ref(_L0_cond_ref(x, itok_B_0_7, L0_cond_weights, fside_8xS_0), L0_attn_Wq, L0_attn_bq, L0_attn_Wk, L0_attn_bk, L0_attn_Wv, L0_attn_bv, L0_attn_Wo, L0_attn_bo)
    x = x + _L0_ffn_ref(_L0_cond2_ref(x, L0_cond2_W, L0_cond2_A, L0_cond2_Bm, L0_cond2_scalings, itok_B_0_6), L0_ffn_w_gate, L0_ffn_wg, L0_ffn_wu, L0_ffn_wd, L0_ffn_sg, L0_ffn_su, L0_ffn_sd)
    return x

_drawn_inputs = setup_inputs


def setup_inputs(seed=0):
    import zlib

    import numpy as np

    out = dict(_drawn_inputs(seed))
    spreads = {'L0_attn_bq': (0.0, 0.272),
     'L0_attn_bk': (0.0, 2.0),
     'L0_attn_bv': (0.0, 0.1),
     'L0_attn_bo': (0.0, 0.1),
     'L0_cond2_scalings': (1.0, 0.6)}
    factors = {'L0_cond2_A': 8.0,
     'L0_cond2_Bm': 8.0,
     'L0_ffn_w_gate': 8.0,
     'L0_ffn_wg': 8.0,
     'L0_ffn_wu': 8.0,
     'L0_ffn_wd': 8.0,
     'L0_ffn_sg': 8.486,
     'L0_ffn_sd': 7.241,
     'L0_ffn_su': 2.671}
    for name, (base, spread) in spreads.items():
        noise = np.random.default_rng([zlib.crc32(name.encode()), seed]).standard_normal(out[name].shape)
        drawn = base * np.exp(spread * noise) if base else spread * noise
        out[name] = jnp.asarray(drawn.astype(out[name].dtype))
    for name, factor in factors.items():
        out[name] = (out[name] * factor).astype(out[name].dtype)
    return out
```

```python
from contextlib import ExitStack

import numpy as np

import concourse.bass as bass
import concourse.mybir as mybir

F32 = mybir.dt.float32
BF16 = mybir.dt.bfloat16
I32 = mybir.dt.int32
U32 = mybir.dt.uint32
ALU = mybir.AluOpType
ACT = mybir.ActivationFunctionType
AX = mybir.AxisListType.X

P = 128
E = 256
S = 32
B = 128
NB = P // S
T = B * S
TILES = T // P
H = 16
D = E // H
KC = E // P
HC = H // KC
XB = 4
SUBJ = 8
RANK = P // 8
MASKED = -1.0e30
NX = 32
F = 128
G = 8
TOP_GROUPS = 3
TOP_K = 6
FC = 2
SLOT_TILES = -(-((T * TOP_K - NX) // P + NX) // 8) * 8
ROWS = T + P
HXW = E + NX
NI = TILES + 1
DCW = P + 2
NDC = -(-NX // 3)


def run_steps(engine, total, head, tail, unroll, body, enter=None):
    assert head % unroll == 0 and (total - tail) % unroll == 0
    for v in range(head):
        if enter and v % unroll == 0:
            enter(v, v)
        body(v, v)
    with engine.Fori(head // unroll, (total - tail) // unroll) as block:
        if enter:
            enter(block * unroll, head)
        for u in range(unroll):
            body(block * unroll + u, head + u)
    for v in range(total - tail, total):
        if enter and v % unroll == 0:
            enter(v, v)
        body(v, v)


def build(nc, x, subj, fside, adapter, wcond, wq, bq, wk, bk, wv, bv, wo, bo, w2, at, scal, bm,
          alibi, headmask, quadmask, acol, ident, wg,
          wgu, wd, sg, su, sd, tri, tail2, tailr, iotas, ecols, pcol, out):
    with ExitStack() as ctx:
        def sb(name, shape, dt=F32):
            return ctx.enter_context(nc.sbuf_tensor(name, shape, dt))

        def pb(name, shape, dt=F32):
            return ctx.enter_context(nc.psum_tensor(name, shape, dt))

        def sem(name):
            return ctx.enter_context(nc.semaphore(name))

        wsel_dram = nc.dram_tensor("wsel", (B, S * S), F32, kind="Internal").ap()
        bsel_dram = nc.dram_tensor("bsel", (B, S), F32, kind="Internal").ap()
        htab = nc.dram_tensor("htab", (ROWS, HXW), F32, kind="Internal").ap()
        acc = [nc.dram_tensor(f"acc{i}", (ROWS, E), F32, kind="Internal").ap() for i in range(2)]

        wgu_sb = sb("wgu_sb", [P, KC, NX, 2 * F])
        wd_sb = sb("wd_sb", [P, NX, E])
        sg_sb, su_sb = sb("sg_sb", [P, KC, FC * P]), sb("su_sb", [P, KC, FC * P])
        sd_sb = sb("sd_sb", [P, FC, E])
        hT = sb("hT", [P, TILES, KC, P])
        lgT = sb("lgT", [P, TILES // 4 * P])
        id_sb = sb("id_sb", [P, P])

        phase_a = ExitStack()

        def sb(name, shape, dt=F32):
            return phase_a.enter_context(nc.sbuf_tensor(name, shape, dt))

        def pb(name, shape, dt=F32):
            return phase_a.enter_context(nc.psum_tensor(name, shape, dt))

        xr = sb("xr", [P, XB, E])
        subj_sb = sb("subj_sb", [P, 1], U32)
        bsel = sb("bsel_sb", [P, S])
        wrow = sb("wrow", [P, TILES, S])
        wbd = sb("wbd", [P, 2, NB, S])
        cb = sb("cb", [P, XB, P])
        wq_sb, wk_sb, wv_sb, wo_sb, w2_sb = (sb(n, [P, KC, E]) for n in ("wq_sb", "wk_sb", "wv_sb", "wo_sb", "w2_sb"))
        bq_sb, bk_sb, bv_sb = (sb(n, [P, KC]) for n in ("bq_sb", "bk_sb", "bv_sb"))
        bo_sb = sb("bo_sb", [P, E])
        at_sb = sb("at_sb", [P, KC, P])
        bm_sb = sb("bm_sb", [P, E])
        scal_sb = sb("scal_sb", [P, 1])
        acol_sb = sb("acol_sb", [P, 1])
        adp_i = sb("adp_i", [P, B], I32)
        adp_f = sb("adp_f", [P, B])
        lmask = sb("lmask", [P, B])
        alibi_sb = sb("alibi_sb", [P, H, S])
        hmask_sb = sb("hmask_sb", [P, HC])
        qmask_sb = sb("qmask_sb", [P, NB])
        cT = sb("cT", [P, KC, P])
        qT = sb("qT", [P, KC, P])
        kT = sb("kT", [P, KC, P])
        kbd = sb("kbd", [P, KC, NB, HC, S])
        early = kbd[:, :, :, :, :].rearrange("p c j h k -> p (c j h k)")
        wsel, zrow = early[:, 0:S * S], early[:, S * S:S * S + HXW]
        vp = sb("vp", [P, 2, H // 2, 2, 2, D])
        sc = sb("sc", [P, H, S])
        mx = sb("mx", [P, H])
        sh = sb("sh", [P, H, S])
        ex = sb("ex", [P, H, S])
        sm = sb("sm", [P, H])
        rs = sb("rs", [P, H])
        pr = sb("pr", [P, H, S])
        pbd = sb("pbd", [P, H, P])
        oT = sb("oT", [P, KC, P])
        x1 = sb("x1", [P, 2, E])
        x1T = sb("x1T", [P, KC, P])
        xam = sb("xam", [P, P])
        hrow = sb("hrow", [P, 2, E])
        hTs = sb("hTs", [P, 2, KC, P])
        wg_sb = sb("wg_sb", [P, KC, 32])

        ps_cv = pb("ps_cv", [P, KC, P])
        ps_k = pb("ps_k", [P, KC, P])
        ps_q = pb("ps_q", [P, KC, P])
        ps_s = pb("ps_s", [P, H * S])
        ps_o = pb("ps_o", [P, 512])
        ps_w = pb("ps_w", [P, E])
        ps_t = pb("ps_t", [P, KC, P])
        ps_a = pb("ps_a", [P, P])

        phase_a.close()

        def sb(name, shape, dt=F32):
            return ctx.enter_context(nc.sbuf_tensor(name, shape, dt))

        tri_sb = sb("tri_sb", [P, 2, DCW], BF16)
        tail2_sb = sb("tail2_sb", [2, NI], BF16)
        tailr_sb = sb("tailr_sb", [2, DCW], BF16)
        io_sb = sb("io_sb", [NI, 2, SLOT_TILES])
        ec_sb = sb("ec_sb", [NX, 4 * NX + 2])
        pcol_sb = sb("pcol_sb", [P, 1])
        one_b = sb("one_b", [P, 2], BF16)
        dc = sb("dc", [NI, NX, DCW], BF16)
        pr_tab = sb("pr_tab", [NI, SLOT_TILES])
        r0_tab = sb("r0_tab", [P, SLOT_TILES])
        e_tab = sb("e_tab", [1, SLOT_TILES], I32)
        sact = sb("sact", [P, 2, FC, 4 * P])
        ssil = sb("ssil", [P, FC, 4 * P])
        sup = sb("sup", [P, FC, 4 * P])
        ys = sb("ys", [P, 4, E])

        routing = ExitStack()

        def sb(name, shape, dt=F32):
            return routing.enter_context(nc.sbuf_tensor(name, shape, dt))

        lmx, lsum, lrs, wsum, wrs = (sb(n, [P, TILES]) for n in ("lmx", "lsum", "lrs", "wsum", "wrs"))
        rt = sb("rt", [P, TILES, NX])
        gs = sb("gs", [P, TILES, G + 5])
        gr = sb("gr", [P, TILES, G + 5])
        m8 = sb("m8", [P, TILES, 8])
        e8 = sb("e8", [P, TILES, 8])
        gmask = sb("gmask", [P, TILES, G])
        ts = sb("ts", [P, TILES, NX + 2])
        tr = sb("tr", [P, TILES, NX + 2])
        sel = sb("sel", [P, TILES, NX])
        selb = sb("selb", [P, NX, TILES + 2], BF16)
        pre = sb("pre", [NX, NI])
        nti = sb("nti", [NX, 2], I32)
        ntf = sb("ntf", [NX, 4])
        e1 = sb("e1", [NX, SLOT_TILES])
        e2 = sb("e2", [NX, SLOT_TILES])
        r0e = sb("r0e", [NX, SLOT_TILES])
        ea = sb("ea", [NX, SLOT_TILES])
        routing.close()
        experts = ExitStack()

        def sb(name, shape, dt=F32):
            return experts.enter_context(nc.sbuf_tensor(name, shape, dt))

        step_sb = sb("step_sb", [NI, 2, P], BF16)
        cnt = sb("cnt", [P, 2])
        cmp = sb("cmp", [P, P])
        idx = sb("idx", [P, 8], U32)
        hx = sb("hx", [P, 4, HXW])
        xT = sb("xT", [P, 2, KC, P])
        sil = sb("sil", [P, 2, F])
        act_x = sb("act_x", [P, 2, F])
        aT = sb("aT", [P, F])
        held = sb("held", [1, 2])
        y = sb("y", [P, 4, E])
        iop = sb("iop", [NI, P])
        experts.close()

        fa = wgu_sb[:, 0, :, :].rearrange("p (k r) n -> p k r n", k=4)
        fb = wgu_sb[:, 1, :, :].rearrange("p (k r) n -> p k r n", k=4)

        def pb(name, shape, dt=F32):
            return psum_s.enter_context(nc.psum_tensor(name, shape, dt))
        psum_s = ExitStack()
        ps_g = [pb(f"ps_g{m}", [P, 512]) for m in range(FC)]
        ps_u = [pb(f"ps_u{m}", [P, 512]) for m in range(FC)]
        ps_d = [pb(f"ps_d{m}", [P, E]) for m in range(2)]
        ps_r = [pb(f"ps_r{m}", [P, 512]) for m in range(2)]
        ps_gu, ps_x, ps_y, ps_i, ps_at = ps_g, ps_u, ps_d, ps_r[0], ps_r[1]
        psum_s.close()

        ld_idx, ld_x, ld_w, ld_m = sem("ld_idx"), [sem(f"ld_x{i}") for i in range(XB)], sem("ld_w"), sem("ld_m")
        got_w, got_b, put_w, put_b, ld_wrow = (sem(n) for n in ("got_w", "got_b", "put_w", "put_b", "ld_wrow"))
        ld_cb = [sem(f"ld_cb{i}") for i in range(XB)]
        zeroed, wbd_ready, adp_ready, lmask_ready = (sem(n) for n in ("zeroed", "wbd_ready", "adp_ready", "lmask_ready"))
        c_done, k_done, q_done, v_done, s_done, o_done, w_done, x1t_done, a_done, h_done, ht_done, g_done = (
            sem(n) for n in ("c_done", "k_done", "q_done", "v_done", "s_done", "o_done", "w_done", "x1t_done",
                             "a_done", "h_done", "ht_done", "g_done"))
        cT_ready, sc_ready, mx_ready, sh_ready, sm_ready, rs_ready, pbd_ready, x1_ready, xam_ready = (
            sem(n) for n in ("cT_ready", "sc_ready", "mx_ready", "sh_ready", "sm_ready", "rs_ready", "pbd_ready",
                             "x1_ready", "xam_ready"))
        k_ready, q_ready, v_ready, ex_ready, oT_ready, x1T_ready, h_ready, hT_ready, g_ready = (
            sem(n) for n in ("k_ready", "q_ready", "v_ready", "ex_ready", "oT_ready", "x1T_ready", "h_ready",
                             "hT_ready", "g_ready"))
        xbo_ready, pr_ready, kbd_ready, hT_kept = sem("xbo_ready"), sem("pr_ready"), sem("kbd_ready"), sem("hT_kept")
        x1_stored = [sem(f"x1_stored{i}") for i in range(2)]
        h_stored = [sem(f"h_stored{i}") for i in range(2)]
        lt_done, lt_read, lsh_ready, lex_ready, w_ready, selb_ready = (
            sem(n) for n in ("lt_done", "lt_read", "lsh_ready", "lex_ready", "w_ready", "selb_ready"))
        rdve, ld_c, rfill, w_stored, dc_done, dc_read, cnt_done, nt_ready, tb_done, e_ready, tabs_done, tabs_ready = (
            sem(n) for n in ("rdve", "ld_c", "rfill", "w_stored", "dc_done", "dc_read", "cnt_done", "nt_ready",
                             "tb_done", "e_ready", "tabs_done", "tabs_ready"))
        held_zero, held_done = sem("held_zero"), sem("held_done")
        ztrash, trashed = sem("ztrash"), sem("trashed")
        ld_s = sem("ld_s")
        ld_e = sem("ld_e")
        sgu_done, ssil_ready, sact_ready, sd_done, ys_ready = (
            sem(n) for n in ("sgu_done", "ssil_ready", "sact_ready", "sd_done", "ys_ready"))
        ys_stored = [sem(f"ys_stored{i}") for i in range(4)]
        step_ready, i_done, cmp_ready, idx_ready, xt_done, xT_ready, gu_done, sil_ready, act_ready, at_done, aT_ready, dn_done, y_ready = (
            sem(n) for n in ("step_ready", "i_done", "cmp_ready", "idx_ready", "xt_done", "xT_ready", "gu_done",
                             "sil_ready", "act_ready", "at_done", "aT_ready", "dn_done", "y_ready"))
        hx_loaded = [sem(f"hx_loaded{i}") for i in range(4)]
        added = [sem(f"added{i}") for i in range(2)]
        ld_f = [sem(f"ld_f{i}") for i in range(4)]
        f_ready, f_stored = sem("f_ready"), sem("f_stored")

        STEPS, HEAD, TAIL = TILES + 3, 4, 3
        NLW, NLM = 7, 12

        def live(s, off):
            return 0 <= s - off < TILES

        GROUPS = TILES // 4
        XSTEPS, XHEAD, XTAIL = SLOT_TILES + 6, 8, 6
        FCH = 4
        FR = T // P // FCH

        def phase_a_over(eng):
            eng.wait_ge(g_ready, TILES)
            eng.wait_ge(hT_kept, TILES)
            for b in range(2):
                eng.wait_ge(x1_stored[b], 16 * TILES // 2)
                eng.wait_ge(h_stored[b], 16 * TILES // 2)

        def alive(s, off):
            return 0 <= s - off < SLOT_TILES

        def experts_window(eng, v, s):
            window = ()
            for at, there in ((v - 8, s >= 8), (v, s < SLOT_TILES)):
                if there:
                    _, values = nc.values_load_multi_w_load_instructions(
                        e_tab[0:1, bass.ds(at, 8)], engines=[eng.engine], min_val=0, max_val=NX - 1,
                        skip_runtime_bounds_check_because="a one-hot over the experts makes them")
                    window += tuple(values)
                else:
                    window += (None,) * 8
            return window

        block = ctx.enter_context(nc.Block())

        @block.sync
        def _(sp):
            sp.dma_start(subj_sb[:, :], subj).then_inc(ld_idx, 16)
            xv = x.rearrange("(i p) e -> p i e", p=P)
            for b in range(XB):
                sp.dma_start(xr[:, b, :], xv[:, b, :]).then_inc(ld_x[b], 16)
            for w, d in ((wk_sb, wk), (wq_sb, wq), (wv_sb, wv), (wo_sb, wo), (w2_sb, w2)):
                sp.dma_start(w[:, :, :], d.rearrange("(c p) n -> p c n", p=P)).then_inc(ld_w, 16)
            sp.dma_start(at_sb[:, :, :], at.rearrange("(c p) n -> p c n", p=P)).then_inc(ld_w, 16)
            sp.dma_start(bm_sb[:, :], bm).then_inc(ld_w, 16)

            for w_, d_ in ((sg_sb, sg), (su_sb, su), (sd_sb, sd)):
                sp.dma_start(w_[:, :, :], d_.rearrange("(c p) n -> p c n", p=P)).then_inc(ld_s, 16)
            sp.wait_ge(put_w, 16)
            sp.dma_start(wrow[:, :, :], wsel_dram.rearrange("(i j) (c d) -> (j c) i d", j=NB, c=S)).then_inc(ld_wrow, 16)
            sp.wait_ge(put_b, 16)
            bias_by_token = bsel_dram.rearrange("b s -> (b s)")
            for b in range(XB):
                sp.dma_start(cb[:, b, :], bias_by_token[b * P:(b + 1) * P].partition_broadcast(P)).then_inc(ld_cb[b], 16)
            sp.wait_ge(ztrash, 1)
            sp.dma_start(htab[T:ROWS, :], zrow[:, :]).then_inc(trashed, 16)
            for a_ in acc:
                sp.dma_start(a_[T:ROWS, :], zrow[:, 0:E]).then_inc(trashed, 16)

            def stores(v, s):
                if live(s, 2):
                    t, b = v - 2, (s - 2) % 2
                    sp.wait_ge(x1_ready, t + 1)
                    sp.dma_start(acc[0][bass.ds(t * P, P), :], x1[:, b, :]).then_inc(x1_stored[b], 16)
                    if live(s, 2 - XB):
                        n = (s - 2) % XB
                        sp.dma_start(xr[:, n, :], x[bass.ds((t + XB) * P, P), :]).then_inc(ld_x[n], 16)
                        sp.dma_start(cb[:, n, :], bias_by_token[bass.ds((t + XB) * P, P)].partition_broadcast(P)).then_inc(ld_cb[n], 16)
                if live(s, 2):
                    t, b = v - 2, (s - 2) % 2
                    sp.wait_ge(h_ready, t + 1)
                    sp.dma_start(htab[bass.ds(t * P, P), 0:E], hrow[:, b, :]).then_inc(h_stored[b], 16)
            run_steps(sp, STEPS, HEAD, TAIL + XB, XB, stores)
            phase_a_over(sp)
            for t_, d_ in ((tri_sb, tri), (tail2_sb, tail2), (tailr_sb, tailr), (io_sb, iotas), (ec_sb, ecols),
                           (pcol_sb, pcol)):
                sp.dma_start(t_[tuple(slice(None) for _ in t_.shape)], d_).then_inc(ld_c, 16)

            def store_weights():
                sp.wait_ge(w_ready, 1)
                sp.dma_start(htab[0:T, E:HXW].rearrange("(i p) e -> p i e", p=P), rt[:, :, :]).then_inc(w_stored, 16)

            def shared_out(v, s):
                for k in range(4):
                    sp.wait_ge(ys_ready, v * 4 + k + 1)
                    sp.dma_start(acc[1][bass.ds(v * 4 * P + k * P, P), :], ys[:, k, :]).then_inc(ys_stored[k], 16)

            for v in range(2):
                shared_out(v, v)
            with sp.Fori(1, (GROUPS - 2) // 2) as two:
                for u in range(2):
                    shared_out(two * 2 + u, 2 + u)
            store_weights()
            for v in range(GROUPS - 2, GROUPS):
                shared_out(v, v)

            for p_ in range(2):
                sp.wait_ge(added[p_], 16 * SLOT_TILES // 2)
            rows = [a_[0:T, :].rearrange("(p r) e -> p r e", p=P) for a_ in acc]
            for k in range(FCH):
                r_ = slice(k * FR, (k + 1) * FR)
                sp.dma_start(fa[:, k, :, :], rows[0][:, r_, :]).then_inc(ld_f[k], 16)
                sp.dma_start(fb[:, k, :, :], rows[1][:, r_, :]).then_inc(ld_f[k], 16)
            for k in range(FCH):
                sp.wait_ge(f_ready, k + 1)
                sp.dma_start(out.rearrange("(p r) e -> p r e", p=P)[:, k * FR:(k + 1) * FR, :], fa[:, k, :, :]).then_inc(f_stored, 16)
            sp.wait_ge(f_stored, 16 * FCH)

        @block.gpsimd
        def _(pool):
            pool.wait_ge(ld_idx, 16)
            pool.indirect_dma_start(wsel[:, :], None, wcond, bass.IndirectOffsetOnAxis(subj_sb[:, 0:1], 0)).then_inc(got_w, 16)
            pool.indirect_dma_start(bsel[:, :], None, fside, bass.IndirectOffsetOnAxis(subj_sb[:, 0:1], 0)).then_inc(got_b, 16)
            pool.memset(vp[:, :, :, :, :, :], 0.0).then_inc(zeroed, 1)
            pool.memset(pbd[:, :, :], 0.0).then_inc(zeroed, 1)
            pool.memset(zrow[:, :], 0.0).then_inc(ztrash, 1)
            pool.wait_ge(ld_m, 16 * NLM)
            pool.wait_ge(trashed, 48)
            pool.wait_ge(ld_wrow, 16)

            def make_wbd(t, n):
                pool.tensor_tensor(wbd[:, n, :, :], wrow[:, bass.ds(t, 1), :].broadcast_to([P, NB, S]),
                                   qmask_sb[:, :, None].broadcast_to([P, NB, S]), ALU.mult).then_inc(wbd_ready, 1)
            make_wbd(0, 0)

            def steps(v, s):
                if live(s, 0):
                    t = v
                    pool.wait_ge(c_done, t + 1)
                    pool.tensor_tensor(xr[:, s % XB, :], xr[:, s % XB, :], bo_sb[:, :], ALU.add).then_inc(xbo_ready, 1)
                    if live(s, -1):
                        make_wbd(t + 1, (s + 1) % 2)
                if live(s, 1):
                    t = v - 1
                    pool.wait_ge(rs_ready, t + 1)
                    if s - 1 >= 1:
                        pool.wait_ge(pbd_ready, t)
                    pool.tensor_tensor(pr[:, :, :], ex[:, :, :], rs[:, :, None].broadcast_to([P, H, S]), ALU.mult).then_inc(pr_ready, 1)
                if live(s, 3):
                    t = v - 3
                    pool.wait_ge(hT_ready, t + 1)
                    pool.tensor_copy(hT[:, bass.ds(t, 1), :, :], hTs[:, (s - 3) % 2, None, :, :]).then_inc(hT_kept, 1)
                if live(s, 0):
                    t = v
                    for c in range(KC):
                        if c == 0:
                            if s >= 1:
                                pool.wait_ge(s_done, t)
                            pool.wait_ge(k_ready, t + 1)
                        pool.tensor_tensor(
                            kbd[:, c, :, :, :],
                            kT[:, c, :].rearrange("p (j k) -> p j k", j=NB)[:, :, None, :].broadcast_to([P, NB, HC, S]),
                            hmask_sb[:, None, :, None].broadcast_to([P, NB, HC, S]), ALU.mult).then_inc(kbd_ready, 1)
            run_steps(pool, STEPS, HEAD, TAIL + XB, XB, steps)

            phase_a_over(pool)
            pool.memset(gs[:, :, :], -1.0).then_inc(rfill, 1)
            pool.memset(ts[:, :, :], -1.0).then_inc(rfill, 1)
            pool.memset(selb[:, :, :], 0.0).then_inc(rfill, 1)
            pool.memset(one_b[:, :], 1.0).then_inc(rfill, 1)

            def shared(v, s):
                for m in range(FC):
                    pool.wait_ge(ssil_ready, v * FC + m + 1)
                    if s >= 2:
                        pool.wait_ge(sd_done, v * 4 - 4)
                    pool.tensor_tensor(sact[:, s % 2, m, :], ssil[:, m, :], sup[:, m, :], ALU.mult).then_inc(sact_ready, 1)
            run_steps(pool, GROUPS, 2, 2, 2, shared)

            def pool_value(value):
                return value if isinstance(value, int) else pool.snap(value)

            pool.memset(held[:, :], 0.0).then_inc(held_zero, 1)
            pool.wait_ge(held_zero, 1)

            def experts_dma(v, s):
                if alive(s, 1):
                    t = v - 1
                    pool.wait_ge(idx_ready, t + 1)
                    if s - 1 >= 4:
                        pool.wait_ge(act_ready, t - 3)
                        pool.wait_ge(xt_done, t - 3)
                if alive(s, 6):
                    t, p_ = v - 6, (s - 6) % 2
                    pool.wait_ge(y_ready, t + 1)
                    if s - 6 >= 2:
                        pool.wait_ge(added[p_], (t - p_) * 8)
                if s >= 1:
                    pool.wait_ge(held_done, v)
                pool.tensor_tensor(held[0:1, 0:1], held[0:1, 1:2], held[0:1, 1:2], ALU.add).then_inc(held_done, 1)
                if alive(s, 6):
                    t, p_ = v - 6, (s - 6) % 2
                    if s - 6 == 1:
                        for k in range(4):
                            pool.wait_ge(ys_stored[k], 16 * GROUPS)
                    pool.wait_ge(trashed, 48)
                    pool.indirect_dma_start(acc[p_], bass.IndirectOffsetOnAxis(idx[:, (s - 6) % 8:(s - 6) % 8 + 1], 0),
                                            y[:, (s - 6) % 4, :], None, compute_op=ALU.add).then_inc(added[p_], 16)
                if alive(s, 1):
                    pool.wait_ge(w_stored, 16)
                    pool.indirect_dma_start(hx[:, (s - 1) % 4, :], None, htab,
                                            bass.IndirectOffsetOnAxis(idx[:, (s - 1) % 8:(s - 1) % 8 + 1], 0)).then_inc(hx_loaded[(s - 1) % 4], 16)
            run_steps(pool, XSTEPS, XHEAD, XTAIL, 8, experts_dma)

        @block.scalar
        def _(act):
            ms = [(bq_sb, bq), (bk_sb, bk), (bv_sb, bv)]
            for t_, d in ms:
                act.dma_start(t_[:, :], d).then_inc(ld_m, 16)
            act.dma_start(hmask_sb[:, :], headmask).then_inc(ld_m, 16)
            act.dma_start(qmask_sb[:, :], quadmask).then_inc(ld_m, 16)
            act.dma_start(bo_sb[:, :], bo.partition_broadcast(P)).then_inc(ld_m, 16)
            act.dma_start(alibi_sb[:, :, :], alibi).then_inc(ld_m, 16)
            act.dma_start(adp_i[:, :], adapter.partition_broadcast(P)).then_inc(ld_m, 16)
            act.dma_start(scal_sb[:, :], scal).then_inc(ld_m, 16)
            act.dma_start(acol_sb[:, :], acol).then_inc(ld_m, 16)
            act.dma_start(id_sb[:, :], ident).then_inc(ld_m, 16)
            act.dma_start(wg_sb[:, :, :], wg.rearrange("(c p) n -> p c n", p=P)).then_inc(ld_m, 16)
            act.wait_ge(got_w, 16)
            act.dma_start(wsel_dram, wsel[:, :]).then_inc(put_w, 16)
            act.wait_ge(got_b, 16)
            act.dma_start(bsel_dram, bsel[:, :]).then_inc(put_b, 16)
            n = NX // 4
            for k in range(4):
                act.dma_start(wgu_sb[:, :, k * n:(k + 1) * n, :],
                              wgu.rearrange("(c p) e n -> p c e n", p=P)[:, :, k * n:(k + 1) * n, :]).then_inc(ld_e, 16)
            act.dma_start(wd_sb[:, :, :], wd.rearrange("e p n -> p e n")).then_inc(ld_e, 16)
            act.wait_ge(ld_m, 16 * NLM)
            act.wait_ge(zeroed, 2)

            def steps(v, s):
                if live(s, 2):
                    t = v - 2
                    act.wait_ge(o_done, t + 1)
                    if s - 2 >= 1:
                        act.wait_ge(w_done, t)
                    for c in range(KC):
                        ins = act.activation(oT[:, c, :], ps_o[:, c * P:(c + 1) * P], ACT.Identity, bias=bv_sb[:, c:c + 1])
                    ins.then_inc(oT_ready, 1)
                if live(s, 1):
                    t = v - 1
                    act.wait_ge(sh_ready, t + 1)
                    if s - 1 >= 1:
                        act.wait_ge(pr_ready, t)
                    act.activation(ex[:, :, :], sh[:, :, :], ACT.Exp).then_inc(ex_ready, 1)
                if live(s, 3):
                    t = v - 3
                    act.wait_ge(ht_done, t + 1)
                    if s - 3 >= 2:
                        act.wait_ge(g_done, t - 1)
                        act.wait_ge(hT_kept, t - 1)
                    act.activation(hTs[:, (s - 3) % 2, :, :], ps_t[:, :, :], ACT.Copy).then_inc(hT_ready, 1)
                if live(s, 0):
                    t = v
                    act.wait_ge(k_done, t + 1)
                    if s >= 1:
                        act.wait_ge(kbd_ready, 2 * t)
                    for c in range(KC):
                        ins = act.activation(kT[:, c, :], ps_k[:, c, :], ACT.Identity, bias=bk_sb[:, c:c + 1])
                    ins.then_inc(k_ready, 1)
                    act.wait_ge(q_done, t + 1)
                    if s >= 1:
                        act.wait_ge(s_done, t)
                    for c in range(KC):
                        ins = act.activation(qT[:, c, :], ps_q[:, c, :], ACT.Identity, bias=bq_sb[:, c:c + 1])
                    ins.then_inc(q_ready, 1)
                    act.wait_ge(v_done, t + 1)
                    if s >= 2:
                        act.wait_ge(o_done, t - 1)
                    for a in range(2):
                        ins = act.activation(vp[:, s % 2, :, a, a, :], ps_cv[:, :, :].rearrange("p c (n a d) -> p (c n) a d", a=2, d=D)[:, :, a, :], ACT.Copy)
                    ins.then_inc(v_ready, 1)
                if live(s, 2):
                    t = v - 2
                    act.wait_ge(x1t_done, t + 1)
                    if s - 2 >= 1:
                        act.wait_ge(h_done, t)
                    act.activation(x1T[:, :, :], ps_t[:, :, :], ACT.Copy).then_inc(x1T_ready, 1)
                if live(s, 3):
                    t, q = v - 3, (s - 3) % 4
                    act.wait_ge(g_done, t + 1)
                    act.activation(lgT[q * 32:(q + 1) * 32, bass.ds((t - q) * 32, P)], ps_o[q * 32:(q + 1) * 32, 0:P], ACT.Copy).then_inc(g_ready, 1)
                if live(s, 2):
                    t, b = v - 2, (s - 2) % 2
                    act.wait_ge(h_done, t + 1)
                    if s - 2 >= 2:
                        act.wait_ge(h_stored[b], (t - b) * 8)
                        act.wait_ge(ht_done, t - 1)
                    act.activation(hrow[:, b, :], ps_w[:, :], ACT.Copy).then_inc(h_ready, 1)
            run_steps(act, STEPS, HEAD, TAIL, XB, steps)

            phase_a_over(act)
            act.wait_ge(lsh_ready, 2)
            act.activation(rt[:, :, :], rt[:, :, :], ACT.Exp).then_inc(lex_ready, 1)

            def shared(v, s):
                if s < GROUPS:
                    for m in range(FC):
                        act.wait_ge(sgu_done, v * FC + m + 1)
                        if s >= 1:
                            act.wait_ge(sact_ready, v * FC + m - 1)
                        act.activation(ssil[:, m, :], ps_g[m][:, :], ACT.Silu)
                        act.activation(sup[:, m, :], ps_u[m][:, :], ACT.Copy).then_inc(ssil_ready, 1)
                if s >= 1:
                    for k in range(4):
                        act.wait_ge(sd_done, v * 4 - 4 + k + 1)
                        if s >= 2:
                            act.wait_ge(ys_stored[k], v * 16 - 16)
                        act.activation(ys[:, k, :], ps_d[k % 2][:, :], ACT.Copy).then_inc(ys_ready, 1)
            run_steps(act, GROUPS + 1, 2, 3, 2, shared)

            def experts_act(v, s):
                if alive(s, 4):
                    t, b = v - 4, (s - 4) % 2
                    act.wait_ge(gu_done, t + 1)
                    if s - 4 >= 2:
                        act.wait_ge(act_ready, t - 1)
                    act.activation(sil[:, b, :], ps_gu[b][:, 0:F], ACT.Silu).then_inc(sil_ready, 1)
                if alive(s, 3):
                    t, b = v - 3, (s - 3) % 2
                    act.wait_ge(xt_done, t + 1)
                    if s - 3 >= 2:
                        act.wait_ge(gu_done, t - 1)
                    act.activation(xT[:, b, :, :].rearrange("p c n -> p (c n)"), ps_x[b][:, 0:E], ACT.Copy).then_inc(xT_ready, 1)
                if alive(s, 5):
                    t = v - 5
                    act.wait_ge(dn_done, t + 1)
                    if s - 5 >= 4:
                        p_ = (s - 5) % 2
                        act.wait_ge(added[p_], (t - p_ - 2) * 8)
                    act.activation(y[:, (s - 5) % 4, :], ps_y[(s - 5) % 2][:, :], ACT.Copy).then_inc(y_ready, 1)
            run_steps(act, XSTEPS, XHEAD, XTAIL, 8, experts_act)

        @block.vector
        def _(dve):
            dve.wait_ge(ld_m, 16 * NLM)
            dve.tensor_copy(adp_f[:, :], adp_i[:, :]).then_inc(adp_ready, 1)
            dve.wait_ge(adp_ready, 1)
            dve.tensor_scalar(lmask[:, :], adp_f[:, :], acol_sb[:, 0:1], scal_sb[:, 0:1], ALU.is_equal, ALU.mult).then_inc(lmask_ready, 1)
            dve.wait_ge(lmask_ready, 1)

            def steps(v, s):
                if live(s, 1):
                    t = v - 1
                    dve.wait_ge(s_done, t + 1)
                    dve.scalar_tensor_tensor(sc[:, :, :].rearrange("p h k -> p (h k)"), ps_s[:, :], float(D) ** -0.5,
                                             alibi_sb[:, :, :].rearrange("p h k -> p (h k)"), ALU.mult, ALU.add).then_inc(sc_ready, 1)
                    dve.wait_ge(sc_ready, t + 1)
                    dve.tensor_reduce(mx[:, :], sc[:, :, :], AX, ALU.max).then_inc(mx_ready, 1)
                    dve.wait_ge(mx_ready, t + 1)
                    if s - 1 >= 1:
                        dve.wait_ge(ex_ready, t)
                    dve.tensor_tensor(sh[:, :, :], sc[:, :, :], mx[:, :, None].broadcast_to([P, H, S]), ALU.subtract).then_inc(sh_ready, 1)
                if live(s, 0):
                    t = v
                    dve.wait_ge(c_done, t + 1)
                    if s >= 1:
                        dve.wait_ge(v_done, t)
                    dve.wait_ge(ld_cb[s % XB], (t - s % XB) * (16 // XB) + 16)
                    dve.tensor_tensor(cT[:, :, :], ps_cv[:, :, :],
                                      cb[:, s % XB, None, :].broadcast_to([P, KC, P]), ALU.add).then_inc(cT_ready, 1)
                if live(s, 1):
                    t = v - 1
                    dve.wait_ge(ex_ready, t + 1)
                    dve.tensor_reduce(sm[:, :], ex[:, :, :], AX, ALU.add).then_inc(sm_ready, 1)
                    dve.wait_ge(sm_ready, t + 1)
                    if s - 1 >= 1:
                        dve.wait_ge(pr_ready, t)
                    dve.reciprocal(rs[:, :], sm[:, :]).then_inc(rs_ready, 1)
                if live(s, 2):
                    t, b = v - 2, (s - 2) % 2
                    dve.wait_ge(w_done, t + 1)
                    dve.wait_ge(xbo_ready, t + 1)
                    if s - 2 >= 2:
                        dve.wait_ge(x1_stored[b], (t - b) * 8)
                        dve.wait_ge(x1t_done, t - 1)
                    dve.tensor_tensor(x1[:, b, :], ps_w[:, :], xr[:, (s - 2) % XB, :], ALU.add).then_inc(x1_ready, 1)
                if live(s, 1):
                    t = v - 1
                    if s - 1 >= 1:
                        dve.wait_ge(o_done, t)
                    dve.wait_ge(pr_ready, t + 1)
                    if s == 1:
                        dve.wait_ge(zeroed, 2)
                    for j in range(NB):
                        q = slice(j * S, (j + 1) * S)
                        dve.transpose(pbd[q, :, q], pr[q, :, :]).then_inc(pbd_ready, 1) if j == NB - 1 else dve.transpose(pbd[q, :, q], pr[q, :, :])
                if live(s, 2):
                    t = v - 2
                    dve.wait_ge(a_done, t + 1)
                    if s - 2 >= 1:
                        dve.wait_ge(h_done, t)
                    dve.tensor_tensor(xam[:, :].rearrange("p (j k) -> p j k", j=NB), ps_a[:, :].rearrange("p (j k) -> p j k", j=NB),
                                      lmask[:, bass.ds(t * NB, NB), None].broadcast_to([P, NB, S]), ALU.mult).then_inc(xam_ready, 1)
            run_steps(dve, STEPS, HEAD, TAIL, XB, steps)

            phase_a_over(dve)
            HT = TILES // 2
            for h_ in range(2):
                dve.wait_ge(lt_done, h_ + 1)
                dve.tensor_reduce(lmx[:, h_ * HT:(h_ + 1) * HT], ps_r[h_][:, :].rearrange("p (i e) -> p i e", e=NX), AX, ALU.max).then_inc(rdve, 1)
            for h_ in range(2):
                dve.wait_ge(rdve, h_ + 1)
                dve.tensor_tensor(rt[:, h_ * HT:(h_ + 1) * HT, :], ps_r[h_][:, :].rearrange("p (i e) -> p i e", e=NX),
                                  lmx[:, h_ * HT:(h_ + 1) * HT, None].broadcast_to([P, HT, NX]), ALU.subtract).then_inc(lsh_ready, 1)
            dve.wait_ge(lex_ready, 1)
            dve.tensor_reduce(lsum[:, :], rt[:, :, :], AX, ALU.add).then_inc(rdve, 1)
            dve.wait_ge(rdve, 3)
            dve.reciprocal(lrs[:, :], lsum[:, :]).then_inc(rdve, 1)
            dve.wait_ge(rdve, 4)
            dve.tensor_tensor(rt[:, :, :], rt[:, :, :], lrs[:, :, None].broadcast_to([P, TILES, NX]), ALU.mult).then_inc(rdve, 1)
            dve.wait_ge(rdve, 5)
            dve.wait_ge(rfill, 4)
            dve.tensor_reduce(gs[:, :, 0:G], rt[:, :, :].rearrange("p i (g k) -> p i g k", g=G), AX, ALU.max).then_inc(rdve, 1)
            dve.wait_ge(rdve, 6)
            for t in range(TILES):
                ins = dve.max(m8[:, t, :], gs[:, t, 0:G])
            ins.then_inc(rdve, 1)
            dve.wait_ge(rdve, 7)
            dve.memset(m8[:, :, TOP_GROUPS:8], -1.0).then_inc(rdve, 1)
            dve.wait_ge(rdve, 8)
            for t in range(TILES):
                ins = dve.match_replace(gr[:, t, :], m8[:, t, :], gs[:, t, :], -2.0)
            ins.then_inc(rdve, 1)
            dve.wait_ge(rdve, 9)
            dve.tensor_scalar(gmask[:, :, :], gr[:, :, 0:G], -2.0, None, ALU.is_equal).then_inc(rdve, 1)
            dve.wait_ge(rdve, 10)
            dve.tensor_tensor(ts[:, :, 0:NX].rearrange("p i (g k) -> p i g k", g=G), rt[:, :, :].rearrange("p i (g k) -> p i g k", g=G),
                              gmask[:, :, :, None].broadcast_to([P, TILES, G, NX // G]), ALU.mult).then_inc(rdve, 1)
            dve.wait_ge(rdve, 11)
            for t in range(TILES):
                ins = dve.max(e8[:, t, :], ts[:, t, 0:NX])
            ins.then_inc(rdve, 1)
            dve.wait_ge(rdve, 12)
            dve.memset(e8[:, :, TOP_K:8], -1.0).then_inc(rdve, 1)
            dve.wait_ge(rdve, 13)
            for t in range(TILES):
                ins = dve.match_replace(tr[:, t, :], e8[:, t, :], ts[:, t, :], -2.0)
            ins.then_inc(rdve, 1)
            dve.wait_ge(rdve, 14)
            dve.tensor_scalar(sel[:, :, :], tr[:, :, 0:NX], -2.0, None, ALU.is_equal).then_inc(rdve, 1)
            dve.wait_ge(rdve, 15)
            dve.tensor_copy(selb[:, :, 1:TILES + 1], sel[:, :, :].rearrange("p i e -> p e i")).then_inc(selb_ready, 1)
            dve.tensor_tensor(rt[:, :, :], ts[:, :, 0:NX], sel[:, :, :], ALU.mult).then_inc(rdve, 1)
            dve.wait_ge(rdve, 16)
            dve.tensor_reduce(wsum[:, :], rt[:, :, :], AX, ALU.add).then_inc(rdve, 1)
            dve.wait_ge(rdve, 17)
            dve.tensor_scalar(wsum[:, :], wsum[:, :], 1e-20, None, ALU.add).then_inc(rdve, 1)
            dve.wait_ge(rdve, 18)
            dve.reciprocal(wrs[:, :], wsum[:, :]).then_inc(rdve, 1)
            dve.wait_ge(rdve, 19)
            dve.tensor_tensor(rt[:, :, :], rt[:, :, :], wrs[:, :, None].broadcast_to([P, TILES, NX]), ALU.mult).then_inc(w_ready, 1)

            for n in range(NDC):
                e_ = range(3 * n, min(3 * n + 3, NX))
                dve.wait_ge(dc_done, n + 1)
                dve.tensor_copy(dc[:, e_[0]:e_[-1] + 1, :], ps_r[n % 2][0:NI, 0:len(e_) * DCW].rearrange("p (e n) -> p e n", n=DCW)).then_inc(dc_read, 1)
            dve.wait_ge(cnt_done, 1)
            dve.wait_ge(ld_c, 96)
            dve.memset(pre[:, 0:1], 0.0).then_inc(rdve, 1)
            dve.tensor_tensor_scan(pre[:, 1:NI], ec_sb[0:NX, 2 * NX:3 * NX], ps_r[NDC % 2][0:NX, 0:TILES], 0.0, ALU.mult, ALU.add).then_inc(rdve, 1)
            dve.wait_ge(rdve, 21)
            dve.tensor_scalar(nti[:, 0:1], pre[:, TILES:NI], float(P - 1), None, ALU.add).then_inc(rdve, 1)
            dve.wait_ge(rdve, 22)
            dve.tensor_scalar(nti[:, 1:2], nti[:, 0:1], 7, None, ALU.arith_shift_right).then_inc(rdve, 1)
            dve.wait_ge(rdve, 23)
            dve.tensor_copy(ntf[:, 0:1], nti[:, 1:2]).then_inc(nt_ready, 1)
            dve.wait_ge(tb_done, 1)
            dve.tensor_copy(ntf[:, 1:2], ps_r[(NDC + 1) % 2][0:NX, 0:1]).then_inc(rdve, 1)
            dve.wait_ge(rdve, 24)
            dve.wait_ge(nt_ready, 1)
            dve.scalar_tensor_tensor(ntf[:, 2:3], ntf[:, 0:1], ntf[:, 1:2], ec_sb[:, 4 * NX + 1:4 * NX + 2], ALU.add, ALU.add).then_inc(rdve, 1)
            dve.tensor_scalar(ntf[:, 3:4], ntf[:, 1:2], float(P), None, ALU.mult).then_inc(rdve, 1)
            dve.tensor_scalar(e1[:, :], io_sb[0:NX, 0, :], ntf[:, 1:2], None, ALU.is_ge).then_inc(rdve, 1)
            dve.wait_ge(rdve, 27)
            dve.scalar_tensor_tensor(e2[:, :], io_sb[0:NX, 0, :], ntf[:, 2:3], e1[:, :], ALU.is_lt, ALU.mult).then_inc(e_ready, 1)
            dve.tensor_scalar(r0e[:, :], io_sb[0:NX, 1, :], ntf[:, 3:4], pre[:, TILES:NI], ALU.subtract, ALU.min).then_inc(rdve, 1)
            dve.wait_ge(rdve, 28)
            dve.wait_ge(e_ready, 1)
            dve.tensor_tensor(ea[:, :], r0e[:, :], e2[:, :], ALU.mult).then_inc(e_ready, 1)
            dve.wait_ge(tabs_done, 1)
            A_, B_ = ps_r[NDC % 2], ps_r[(NDC + 1) % 2]
            dve.tensor_copy(pr_tab[:, :], A_[0:NI, 0:SLOT_TILES]).then_inc(tabs_ready, 1)
            dve.tensor_copy(e_tab[:, :], A_[0:1, 256:256 + SLOT_TILES]).then_inc(tabs_ready, 1)
            dve.tensor_scalar(r0_tab[:, :], B_[:, 0:SLOT_TILES], pcol_sb[:, 0:1], None, ALU.add).then_inc(tabs_ready, 1)
            dve.tensor_copy(iop[:, :], io_sb[0:NI, 0, 0:P]).then_inc(tabs_ready, 1)
            dve.wait_ge(tabs_ready, 4)
            dve.wait_ge(w_stored, 16)
            regs = {}

            def experts_of(v, s):
                regs["e"] = experts_window(dve, v, s)

            def expert(s, off):
                return regs["e"][8 + s % 8 - off]

            def experts_dve(v, s):
                if alive(s, 0):
                    t = v
                    if s >= 2:
                        dve.wait_ge(i_done, t - 1)
                    dve.tensor_scalar(step_sb[:, s % 2, :], iop[:, :], pr_tab[:, bass.ds(t, 1)], None, ALU.is_ge).then_inc(step_ready, 1)
                if alive(s, 5):
                    t = v - 5
                    dve.wait_ge(at_done, t + 1)
                    if s - 5 >= 1:
                        dve.wait_ge(dn_done, t)
                    dve.tensor_copy(aT[:, :], ps_at[:, 0:P]).then_inc(aT_ready, 1)
                if alive(s, 4):
                    t, b = v - 4, (s - 4) % 2
                    dve.wait_ge(sil_ready, t + 1)
                    if s - 4 >= 2:
                        dve.wait_ge(at_done, t - 1)
                    dve.scalar_tensor_tensor(act_x[:, b, :], sil[:, b, :], hx[:, (s - 4) % 4, bass.ds(expert(s, 4) + E, 1)],
                                             ps_gu[b][:, F:2 * F], ALU.mult, ALU.mult).then_inc(act_ready, 1)
                if alive(s, 0):
                    t = v
                    dve.wait_ge(i_done, t + 1)
                    if s >= 1:
                        dve.wait_ge(idx_ready, t)
                    dve.tensor_scalar(cmp[:, :], ps_i[:, 0:P], r0_tab[:, bass.ds(t, 1)], 0.0, ALU.is_le, ALU.add,
                                      accum_out=cnt[:, s % 2:s % 2 + 1]).then_inc(cmp_ready, 1)
                    dve.wait_ge(cmp_ready, t + 1)
                    if s >= 8:
                        dve.wait_ge(hx_loaded[s % 4], (t - s % 4) * 4 - 16)
                        dve.wait_ge(added[s % 2], (t - s % 2) * 8 - 48)
                    dve.tensor_tensor(idx[:, s % 8:s % 8 + 1], ps_i[:, P:P + 1], cnt[:, s % 2:s % 2 + 1], ALU.add).then_inc(idx_ready, 1)
            run_steps(dve, XSTEPS, XHEAD, XTAIL, 8, experts_dve, experts_of)

            for k in range(FCH):
                dve.wait_ge(ld_f[k], 32)
                dve.tensor_tensor(fa[:, k, :, :], fa[:, k, :, :], fb[:, k, :, :], ALU.add).then_inc(f_ready, 1)

        @block.tensor
        def _(pe):
            pe.wait_ge(ld_w, 16 * NLW)
            pe.wait_ge(ld_m, 16 * NLM)

            def steps(v, s):
                if live(s, 1):
                    t = v - 1
                    pe.wait_ge(kbd_ready, 2 * t + 2)
                    if s - 1 >= 1:
                        pe.wait_ge(sc_ready, t)
                    pe.wait_ge(q_ready, t + 1)
                    for c in range(KC):
                        for j in range(NB):
                            ins = pe.matmul(ps_s[j * S:(j + 1) * S, c * HC * S:(c + 1) * HC * S], qT[:, c, j * S:(j + 1) * S],
                                            kbd[:, c, j, :, :].rearrange("p h k -> p (h k)"), start=True, stop=True)
                    ins.then_inc(s_done, 1)
                if live(s, 2):
                    t, b = v - 2, (s - 2) % 2
                    if s - 2 >= 2:
                        pe.wait_ge(g_ready, t - 1)
                    pe.wait_ge(pbd_ready, t + 1)
                    pe.wait_ge(v_ready, t + 1)
                    for c in range(KC):
                        for a in range(2):
                            for g in range(NB):
                                pair = c * NB + g
                                ins = pe.matmul(ps_o[g * S:(g + 1) * S, c * P:(c + 1) * P], vp[:, b, pair, a, :, :].rearrange("p a d -> p (a d)"),
                                                pbd[:, 2 * pair + a, :], start=(a == 0), stop=(a == 1))
                    ins.then_inc(o_done, 1)
                if live(s, 0):
                    t = v
                    if s >= 1:
                        pe.wait_ge(v_ready, t)
                    pe.wait_ge(wbd_ready, t + 1)
                    pe.wait_ge(ld_x[s % XB], (t - s % XB) * (16 // XB) + 16)
                    for c in range(KC):
                        ins = pe.matmul(ps_cv[:, c, :], xr[:, s % XB, c * P:(c + 1) * P], wbd[:, s % 2, :, :].rearrange("p j d -> p (j d)"), start=True, stop=True)
                    ins.then_inc(c_done, 1)
                if live(s, 3):
                    t, b = v - 3, (s - 3) % 2
                    pe.wait_ge(h_ready, t + 1)
                    pe.wait_ge(x1T_ready, t + 1)
                    for c in range(KC):
                        ins = pe.transpose(ps_t[:, c, :], hrow[:, b, c * P:(c + 1) * P], id_sb[:, :])
                    ins.then_inc(ht_done, 1)
                if live(s, 2):
                    t = v - 2
                    if s - 2 >= 1:
                        pe.wait_ge(h_ready, t)
                    pe.wait_ge(oT_ready, t + 1)
                    for c in range(KC):
                        ins = pe.matmul(ps_w[:, :], oT[:, c, :], wo_sb[:, c, :], start=(c == 0), stop=(c == KC - 1))
                    ins.then_inc(w_done, 1)
                if live(s, 0):
                    t = v
                    if s >= 1:
                        pe.wait_ge(q_ready, t)
                    pe.wait_ge(cT_ready, t + 1)
                    for w, ps, done in ((wk_sb, ps_k, k_done), (wq_sb, ps_q, q_done)):
                        for m in range(KC):
                            for c in range(KC):
                                ins = pe.matmul(ps[:, m, :], w[:, c, m * P:(m + 1) * P], cT[:, c, :], start=(c == 0), stop=(c == KC - 1))
                        ins.then_inc(done, 1)
                    for c in range(KC):
                        ins = pe.matmul(ps_cv[:, :, :].rearrange("p c n -> p (c n)"), cT[:, c, :], wv_sb[:, c, :], start=(c == 0), stop=(c == KC - 1))
                    ins.then_inc(v_done, 1)
                if live(s, 2):
                    t, b = v - 2, (s - 2) % 2
                    pe.wait_ge(x1_ready, t + 1)
                    if s - 2 >= 1:
                        pe.wait_ge(hT_ready, t)
                    for c in range(KC):
                        ins = pe.transpose(ps_t[:, c, :], x1[:, b, c * P:(c + 1) * P], id_sb[:, :])
                    ins.then_inc(x1t_done, 1)
                if live(s, 3):
                    t, q = v - 3, (s - 3) % 4
                    if s - 3 < TILES - 1:
                        pe.wait_ge(oT_ready, t + 2)
                    pe.wait_ge(hT_ready, t + 1)
                    for c in range(KC):
                        ins = pe.matmul(ps_o[q * 32:(q + 1) * 32, 0:P], wg_sb[:, c, :], hTs[:, (s - 3) % 2, c, :], start=(c == 0), stop=(c == KC - 1))
                    ins.then_inc(g_done, 1)
                if live(s, 2):
                    t = v - 2
                    if s - 2 >= 1:
                        pe.wait_ge(xam_ready, t)
                    pe.wait_ge(x1T_ready, t + 1)
                    for c in range(KC):
                        ins = pe.matmul(ps_a[:, :], at_sb[:, c, :], x1T[:, c, :], start=(c == 0), stop=(c == KC - 1))
                    ins.then_inc(a_done, 1)
                    for c in range(KC):
                        pe.matmul(ps_w[:, :], x1T[:, c, :], w2_sb[:, c, :], start=(c == 0), stop=False)
                    pe.wait_ge(xam_ready, t + 1)
                    pe.matmul(ps_w[:, :], xam[:, :], bm_sb[:, :], start=False, stop=True).then_inc(h_done, 1)
            run_steps(pe, STEPS, HEAD, TAIL, XB, steps)

            phase_a_over(pe)
            for a_ in range(TILES // 4):
                ins = pe.transpose(ps_r[a_ // 4][:, (a_ % 4) * P:(a_ % 4 + 1) * P], lgT[:, a_ * P:(a_ + 1) * P], id_sb[:, :])
                if a_ % 4 == 3:
                    ins.then_inc(lt_done, 1)
            pe.wait_ge(ld_s, 48)

            def shared(v, s):
                if s < GROUPS:
                    for m in range(FC):
                        if s >= 1:
                            pe.wait_ge(ssil_ready, v * FC + m - 1)
                        for w_, ps in ((sg_sb, ps_g), (su_sb, ps_u)):
                            for c in range(KC):
                                ins = pe.matmul(ps[m][:, :], w_[:, c, m * P:(m + 1) * P], hT[:, bass.ds(v * 4, 4), c, :], start=(c == 0), stop=(c == KC - 1))
                        ins.then_inc(sgu_done, 1)
                if s >= 1:
                    pe.wait_ge(sact_ready, v * FC)
                    for k in range(4):
                        if s >= 2 or k >= 2:
                            pe.wait_ge(ys_ready, v * 4 - 4 + k - 1)
                        for m in range(FC):
                            ins = pe.matmul(ps_d[k % 2][:, :], sact[:, (s - 1) % 2, m, k * P:(k + 1) * P], sd_sb[:, m, :], start=(m == 0), stop=(m == FC - 1))
                        ins.then_inc(sd_done, 1)

            def running_counts():
                pe.wait_ge(selb_ready, 1)
                pe.wait_ge(ld_c, 96)
                for n in range(NDC):
                    if n >= 2:
                        pe.wait_ge(dc_read, n - 1)
                    for k, e_ in enumerate(range(3 * n, min(3 * n + 3, NX))):
                        o_ = ps_r[n % 2][0:NI, k * DCW:(k + 1) * DCW]
                        pe.matmul(o_, selb[:, e_, 1:NI + 1], tri_sb[:, 0, :], start=True, stop=False)
                        pe.matmul(o_, selb[:, e_, 0:NI], tri_sb[:, 1, :], start=False, stop=False)
                        ins = pe.matmul(o_, tail2_sb[:, :], tailr_sb[:, :], start=False, stop=True)
                    ins.then_inc(dc_done, 1)
                pe.wait_ge(dc_read, NDC - 1)
                for t in range(TILES):
                    ins = pe.matmul(ps_r[NDC % 2][0:NX, t:t + 1], selb[:, :, t + 1], one_b[:, 0:1], start=True, stop=True)
                ins.then_inc(cnt_done, 1)

            def first_tiles():
                pe.wait_ge(nt_ready, 1)
                pe.wait_ge(dc_read, NDC)
                pe.matmul(ps_r[(NDC + 1) % 2][0:NX, 0:1], ec_sb[0:NX, 0:NX], ntf[:, 0:1], start=True, stop=True).then_inc(tb_done, 1)

            def slot_tables():
                pe.wait_ge(e_ready, 2)
                A_, B_ = ps_r[NDC % 2], ps_r[(NDC + 1) % 2]
                pe.matmul(A_[0:NI, 0:SLOT_TILES], pre[:, :], e2[:, :], start=True, stop=False)
                pe.matmul(A_[0:NI, 0:SLOT_TILES], ec_sb[0:NX, 3 * NX:4 * NX + 1][:, 0:NI], ea[:, :], start=False, stop=True)
                pe.matmul(A_[0:NX, 256:256 + SLOT_TILES], ec_sb[0:NX, NX:2 * NX], e2[:, :], start=True, stop=True)
                for q in range(4):
                    ins = pe.matmul(B_[q * 32:(q + 1) * 32, 0:SLOT_TILES], ec_sb[0:NX, 2 * NX:3 * NX], ea[:, :], start=True, stop=True)
                ins.then_inc(tabs_done, 1)

            for v in range(2):
                shared(v, v)
            with pe.Fori(1, (GROUPS - 2) // 2) as two:
                for u in range(2):
                    shared(two * 2 + u, 2 + u)
            running_counts()
            shared(GROUPS - 2, GROUPS - 2)
            first_tiles()
            shared(GROUPS - 1, GROUPS - 1)
            slot_tables()
            shared(GROUPS, GROUPS)
            pe.wait_ge(tabs_ready, 4)
            pe.wait_ge(ld_e, 80)
            pe.wait_ge(ys_ready, 4 * GROUPS)
            regs = {}

            def experts_of(v, s):
                regs["e"] = experts_window(pe, v, s)

            def expert(s, off):
                return regs["e"][8 + s % 8 - off]

            def experts_pe(v, s):
                if alive(s, 4):
                    t, b = v - 4, (s - 4) % 2
                    pe.wait_ge(xT_ready, t + 1)
                    if s - 4 >= 2:
                        pe.wait_ge(act_ready, t - 1)
                    for c in range(KC):
                        ins = pe.matmul(ps_gu[b][:, 0:2 * F], xT[:, b, c, :], wgu_sb[:, c, bass.ds(expert(s, 4), 1), :].rearrange("p e n -> p (e n)"), start=(c == 0), stop=(c == KC - 1))
                    ins.then_inc(gu_done, 1)
                if alive(s, 5):
                    t, b = v - 5, (s - 5) % 2
                    pe.wait_ge(act_ready, t + 1)
                    if s - 5 >= 1:
                        pe.wait_ge(aT_ready, t)
                    pe.transpose(ps_at[:, 0:P], act_x[:, b, :], id_sb[:, :]).then_inc(at_done, 1)
                if alive(s, 3):
                    t, b = v - 3, (s - 3) % 2
                    pe.wait_ge(hx_loaded[(s - 3) % 4], (t - (s - 3) % 4) * 4 + 16)
                    if s - 3 >= 2:
                        pe.wait_ge(xT_ready, t - 1)
                    for c in range(KC):
                        ins = pe.transpose(ps_x[b][:, c * P:(c + 1) * P], hx[:, (s - 3) % 4, c * P:(c + 1) * P], id_sb[:, :])
                    ins.then_inc(xt_done, 1)
                if alive(s, 0):
                    t = v
                    pe.wait_ge(step_ready, t + 1)
                    if s >= 1:
                        pe.wait_ge(idx_ready, t)
                    pe.matmul(ps_i[:, 0:DCW], step_sb[:, s % 2, :], dc[:, bass.ds(expert(s, 0), 1), :].rearrange("p e n -> p (e n)"), start=True, stop=True).then_inc(i_done, 1)
                if alive(s, 5):
                    t, b = v - 5, (s - 5) % 2
                    pe.wait_ge(aT_ready, t + 1)
                    if s - 5 >= 2:
                        pe.wait_ge(y_ready, t - 1)
                    pe.matmul(ps_y[b][:, :], aT[:, :], wd_sb[:, bass.ds(expert(s, 5), 1), :].rearrange("p e n -> p (e n)"), start=True, stop=True).then_inc(dn_done, 1)
            run_steps(pe, XSTEPS, XHEAD, XTAIL, 8, experts_pe, experts_of)


def kernel(**inputs):
    import concourse.bacc as bacc
    from concourse.bass_utils import run_bass_kernel_spmd

    c = np.ascontiguousarray
    given = {k: np.asarray(v) for k, v in inputs.items()}
    attn = {k[8:]: v for k, v in given.items() if k.startswith("L0_attn_")}
    cond2 = {k[9:]: v for k, v in given.items() if k.startswith("L0_cond2_")}
    ffn = {k[7:]: v for k, v in given.items() if k.startswith("L0_ffn_")}

    def column(bias):
        return c(bias.reshape(KC, P).T)

    arrays = dict(
        x=c(given["x"].reshape(T, E)), subj=c(given["itok_B_0_7"].reshape(B, 1)).view(np.uint32),
        fside=c(given["fside_8xS_0"]), adapter=c(given["itok_B_0_6"]),
        wcond=c(given["L0_cond_weights"].reshape(SUBJ, S * S)),
        wq=c(attn["Wq"].T), bq=column(attn["bq"]), wk=c(attn["Wk"].T), bk=column(attn["bk"]),
        wv=c(attn["Wv"].T), bv=column(attn["bv"]), wo=c(attn["Wo"].T), bo=c(attn["bo"]),
        w2=c(cond2["W"].T), at=c(cond2["A"].reshape(P, E).T), scal=c(np.repeat(cond2["scalings"], RANK).reshape(P, 1)),
        bm=c(cond2["Bm"].transpose(0, 2, 1).reshape(P, E)), wg=c(ffn["w_gate"].T),
        wgu=c(np.concatenate([ffn["wg"], ffn["wu"]], 2).transpose(1, 0, 2)), wd=c(ffn["wd"]),
        sg=c(ffn["sg"].T), su=c(ffn["su"].T), sd=c(ffn["sd"].T), **shape_tables())

    nc = bacc.Bacc("TRN2", target_bir_lowering=False, num_devices=1)
    aps = {name: nc.dram_tensor(name, a.shape, mybir.dt.from_np(a.dtype), kind="ExternalInput").ap()
           for name, a in arrays.items()}
    aps["out"] = nc.dram_tensor("out", (T, E), F32, kind="ExternalOutput").ap()
    build(nc, **aps)
    result = run_bass_kernel_spmd(nc, [arrays], core_ids=[0])
    return np.asarray(result.results[0]["out"]).reshape(B, S, E)


def shape_tables():
    bf16 = mybir.dt.np(BF16)
    p, e, j = np.arange(P), np.arange(NX), np.arange(SLOT_TILES)
    slopes = np.array([2.0 ** (-8.0 * (h + 1) / H) for h in range(H)], np.float32)
    query, key = p % S, np.arange(S)
    distance = np.abs(key[None, :] - query[:, None]).astype(np.float32)
    alibi = -slopes[None, :, None] * distance[:, None, :]
    alibi = np.where((key[None, :] > query[:, None])[:, None, :], np.float32(MASKED), alibi)
    tri = np.zeros((P, 2, DCW), np.float32)
    tri[:, 0, :P] = p[:, None] <= p[None, :]
    tri[:, 1, :P] = p[:, None] > p[None, :]
    tail2, tailr = np.zeros((2, NI), np.float32), np.zeros((2, DCW), np.float32)
    tail2[0, NI - 1], tail2[1, 1:] = 1, 1
    tailr[0, :P], tailr[1, P] = p + 1, P
    ecols = np.zeros((NX, 4 * NX + 2), np.float32)
    ecols[:, 0:NX] = e[:, None] < e[None, :]
    ecols[:, NX:2 * NX] = e[:, None]
    ecols[:, 2 * NX:3 * NX] = 1
    ecols[:, 3 * NX:4 * NX + 1] = -1
    ecols[NX - 1, 4 * NX + 1] = 1e6
    return dict(alibi=alibi, ident=np.eye(P, dtype=np.float32),
                headmask=(p[:, None] // D == np.arange(HC)).astype(np.float32),
                quadmask=(p[:, None] // S == np.arange(NB)).astype(np.float32),
                acol=(p // RANK).astype(np.float32).reshape(P, 1), pcol=p.astype(np.float32).reshape(P, 1),
                tri=tri.astype(bf16), tail2=tail2.astype(bf16), tailr=tailr.astype(bf16),
                iotas=np.ascontiguousarray(np.broadcast_to(np.stack([j, P * j]).astype(np.float32), (NI, 2, SLOT_TILES))),
                ecols=ecols)
```

```python
from contextlib import ExitStack

import numpy as np

import concourse.bass as bass
import concourse.mybir as mybir

F32 = mybir.dt.float32
BF16 = mybir.dt.bfloat16
I32 = mybir.dt.int32
U32 = mybir.dt.uint32
ALU = mybir.AluOpType
ACT = mybir.ActivationFunctionType
AX = mybir.AxisListType.X

P = 128
E = 256
S = 32
B = 128
NB = P // S
T = B * S
TILES = T // P
H = 16
D = E // H
KC = E // P
HC = H // KC
XB = 4
SUBJ = 8
RANK = 16
MASKED = -1.0e30
NX = 32
F = 128
G = 8
TOP_GROUPS = 3
TOP_K = 6
FC = 2
SLOT_TILES = -(-((T * TOP_K - NX) // P + NX) // 16) * 16
ROWS = T + P
HXW = E + NX
NI = TILES + 1
DCW = P + 2
NDC = -(-NX // 3)


def run_steps(engine, total, head, tail, unroll, body, enter=None):
    assert head % unroll == 0 and (total - tail) % unroll == 0
    for v in range(head):
        if enter and v % unroll == 0:
            enter(v, v)
        body(v, v)
    with engine.Fori(head // unroll, (total - tail) // unroll) as block:
        if enter:
            enter(block * unroll, head)
        for u in range(unroll):
            body(block * unroll + u, head + u)
    for v in range(total - tail, total):
        if enter and v % unroll == 0:
            enter(v, v)
        body(v, v)


def forward(nc, x, subj, fside, adapter, wcond, wq, bq, wk, bk, wv, bv, wo, bo, w2, at, scal, bm,
            alibi, headmask, quadmask, acol, ident, wg,
            wgu, wd, sg, su, sd, tri, tail2, tailr, iotas, ecols, pcol, out):
    with ExitStack() as ctx:
        def sb(name, shape, dt=F32):
            return ctx.enter_context(nc.sbuf_tensor(name, shape, dt))

        def pb(name, shape, dt=F32):
            return ctx.enter_context(nc.psum_tensor(name, shape, dt))

        def sem(name):
            return ctx.enter_context(nc.semaphore(name))

        wsel_dram = nc.dram_tensor("wsel", (B, S * S), F32, kind="Internal").ap()
        bsel_dram = nc.dram_tensor("bsel", (B, S), F32, kind="Internal").ap()
        htab = nc.dram_tensor("htab", (ROWS, HXW), F32, kind="Internal").ap()
        acc = [nc.dram_tensor(f"acc{i}", (ROWS, E), F32, kind="Internal").ap() for i in range(2)]

        wgu_sb = sb("wgu_sb", [P, KC, NX, 2 * F])
        wd_sb = sb("wd_sb", [P, NX, E])
        sg_sb, su_sb = sb("sg_sb", [P, KC, FC * P]), sb("su_sb", [P, KC, FC * P])
        sd_sb = sb("sd_sb", [P, FC, E])
        hT = sb("hT", [P, TILES, KC, P])
        lgT = sb("lgT", [P, TILES // 4 * P])
        id_sb = sb("id_sb", [P, P])
        zrow = sb("zrow", [P, HXW])

        phase_a = ExitStack()

        def sb(name, shape, dt=F32):
            return phase_a.enter_context(nc.sbuf_tensor(name, shape, dt))

        def pb(name, shape, dt=F32):
            return phase_a.enter_context(nc.psum_tensor(name, shape, dt))

        xr = sb("xr", [P, XB, E])
        subj_sb = sb("subj_sb", [P, 1], U32)
        bsel = sb("bsel_sb", [P, S])
        wrow = sb("wrow", [P, TILES, S])
        wbd = sb("wbd", [P, 2, NB, S])
        cb = sb("cb", [P, XB, P])
        wq_sb, wk_sb, wv_sb, wo_sb, w2_sb = (sb(n, [P, KC, E]) for n in ("wq_sb", "wk_sb", "wv_sb", "wo_sb", "w2_sb"))
        bq_sb, bk_sb, bv_sb = (sb(n, [P, KC]) for n in ("bq_sb", "bk_sb", "bv_sb"))
        bo_sb = sb("bo_sb", [P, E])
        at_sb = sb("at_sb", [P, KC, P])
        bm_sb = sb("bm_sb", [P, E])
        scal_sb = sb("scal_sb", [P, 1])
        acol_sb = sb("acol_sb", [P, 1])
        adp_i = sb("adp_i", [P, B], I32)
        adp_f = sb("adp_f", [P, B])
        lmask = sb("lmask", [P, B])
        alibi_sb = sb("alibi_sb", [P, H, S])
        hmask_sb = sb("hmask_sb", [P, HC])
        qmask_sb = sb("qmask_sb", [P, NB])
        cT = sb("cT", [P, KC, P])
        qT = sb("qT", [P, KC, P])
        kT = sb("kT", [P, KC, P])
        kbd = sb("kbd", [P, KC, NB, HC, S])
        early = kbd[:, :, :, :, :].rearrange("p c j h k -> p (c j h k)")
        wsel = early[:, 0:S * S]
        vp = sb("vp", [P, 2, H // 2, 2, 2, D])
        sc = sb("sc", [P, H, S])
        mx = sb("mx", [P, H])
        sh = sb("sh", [P, H, S])
        ex = sb("ex", [P, H, S])
        sm = sb("sm", [P, H])
        rs = sb("rs", [P, H])
        pr = sb("pr", [P, H, S])
        pbd = sb("pbd", [P, H, P])
        oT = sb("oT", [P, KC, P])
        x1 = sb("x1", [P, 2, E])
        x1T = sb("x1T", [P, KC, P])
        xam = sb("xam", [P, P])
        hrow = sb("hrow", [P, 2, E])
        hTs = sb("hTs", [P, 2, KC, P])
        wg_sb = sb("wg_sb", [P, KC, 32])

        ps_cv = pb("ps_cv", [P, KC, P])
        ps_k = pb("ps_k", [P, KC, P])
        ps_q = pb("ps_q", [P, KC, P])
        ps_s = pb("ps_s", [P, H * S])
        ps_o = pb("ps_o", [P, 512])
        ps_w = pb("ps_w", [P, E])
        ps_t = pb("ps_t", [P, KC, P])
        ps_a = pb("ps_a", [P, P])

        phase_a.close()

        def sb(name, shape, dt=F32):
            return ctx.enter_context(nc.sbuf_tensor(name, shape, dt))

        tri_sb = sb("tri_sb", [P, 2, DCW], BF16)
        tail2_sb = sb("tail2_sb", [2, NI], BF16)
        tailr_sb = sb("tailr_sb", [2, DCW], BF16)
        io_sb = sb("io_sb", [NI, 2, SLOT_TILES])
        ec_sb = sb("ec_sb", [NX, 4 * NX + 2])
        pcol_sb = sb("pcol_sb", [P, 1])
        one_b = sb("one_b", [P, 2], BF16)
        dc = sb("dc", [NI, NX, DCW], BF16)
        pr_tab = sb("pr_tab", [NI, SLOT_TILES])
        r0_tab = sb("r0_tab", [P, SLOT_TILES])
        e_tab = sb("e_tab", [1, SLOT_TILES], I32)
        ssil = sb("ssil", [P, FC * P])
        sact = sb("sact", [P, FC * P])

        routing = ExitStack()

        def sb(name, shape, dt=F32):
            return routing.enter_context(nc.sbuf_tensor(name, shape, dt))

        lmx, lsum, lrs, wsum, wrs = (sb(n, [P, TILES]) for n in ("lmx", "lsum", "lrs", "wsum", "wrs"))
        rt = sb("rt", [P, TILES, NX])
        gs = sb("gs", [P, TILES, G + 5])
        gr = sb("gr", [P, TILES, G + 5])
        m8 = sb("m8", [P, TILES, 8])
        e8 = sb("e8", [P, TILES, 8])
        gmask = sb("gmask", [P, TILES, G])
        ts = sb("ts", [P, TILES, NX + 2])
        tr = sb("tr", [P, TILES, NX + 2])
        sel = sb("sel", [P, TILES, NX])
        selb = sb("selb", [P, NX, TILES + 2], BF16)
        pre = sb("pre", [NX, NI])
        nti = sb("nti", [NX, 2], I32)
        ntf = sb("ntf", [NX, 4])
        e1 = sb("e1", [NX, SLOT_TILES])
        e2 = sb("e2", [NX, SLOT_TILES])
        r0e = sb("r0e", [NX, SLOT_TILES])
        ea = sb("ea", [NX, SLOT_TILES])
        routing.close()
        experts = ExitStack()

        def sb(name, shape, dt=F32):
            return experts.enter_context(nc.sbuf_tensor(name, shape, dt))

        step_sb = sb("step_sb", [NI, 2, P], BF16)
        cnt = sb("cnt", [P, 2])
        cmp = sb("cmp", [P, P])
        idx = sb("idx", [P, 8], U32)
        hx = sb("hx", [P, 8, HXW])
        xa = sb("xa", [P, 2, E + F])
        sidx = sb("sidx", [P, 8], U32)
        sil = sb("sil", [P, 2, F])
        act_x = sb("act_x", [P, 4, F])
        y = sb("y", [P, 4, E])
        iop = sb("iop", [NI, P])
        experts.close()

        fa, fb = wgu_sb[:, 0, :, :], wgu_sb[:, 1, :, :]
        h_flat = hT[:, :, :, :].rearrange("p i c n -> p (i c n)")

        def pb(name, shape, dt=F32):
            return psum_s.enter_context(nc.psum_tensor(name, shape, dt))
        psum_s = ExitStack()
        ps_gu = [pb(f"ps_gu{i}", [P, 512]) for i in range(2)]
        ps_x = [pb(f"ps_x{i}", [P, 512]) for i in range(2)]
        ps_y = [pb(f"ps_y{i}", [P, 512]) for i in range(2)]
        ps_i = pb("ps_i", [P, 256])
        ps_sh = pb("ps_sh", [P, 4 * P])
        early_banks = [ps_sh, ps_y[0], ps_y[1], ps_x[1]]
        ps_r = ps_gu + ps_x
        psum_s.close()

        ld_q, ld_o = sem("ld_q"), sem("ld_o")
        ld_idx, ld_x, ld_w, ld_m = sem("ld_idx"), [sem(f"ld_x{i}") for i in range(XB)], sem("ld_w"), sem("ld_m")
        got_w, got_b, put_w, put_b, ld_wrow = (sem(n) for n in ("got_w", "got_b", "put_w", "put_b", "ld_wrow"))
        ld_cb = [sem(f"ld_cb{i}") for i in range(XB)]
        zeroed, wbd_ready, adp_ready, lmask_ready = (sem(n) for n in ("zeroed", "wbd_ready", "adp_ready", "lmask_ready"))
        c_done, k_done, q_done, v_done, s_done, o_done, w_done, x1t_done, a_done, h_done, ht_done, g_done = (
            sem(n) for n in ("c_done", "k_done", "q_done", "v_done", "s_done", "o_done", "w_done", "x1t_done",
                             "a_done", "h_done", "ht_done", "g_done"))
        cT_ready, sc_ready, mx_ready, sh_ready, sm_ready, rs_ready, pbd_ready, x1_ready, xam_ready = (
            sem(n) for n in ("cT_ready", "sc_ready", "mx_ready", "sh_ready", "sm_ready", "rs_ready", "pbd_ready",
                             "x1_ready", "xam_ready"))
        k_ready, q_ready, v_ready, ex_ready, oT_ready, x1T_ready, h_ready, hT_ready, g_ready = (
            sem(n) for n in ("k_ready", "q_ready", "v_ready", "ex_ready", "oT_ready", "x1T_ready", "h_ready",
                             "hT_ready", "g_ready"))
        xbo_ready, pr_ready, kbd_ready, hT_kept = sem("xbo_ready"), sem("pr_ready"), sem("kbd_ready"), sem("hT_kept")
        x1_stored = [sem(f"x1_stored{i}") for i in range(2)]
        h_stored = [sem(f"h_stored{i}") for i in range(2)]
        lt_done, lsh_ready, lex_ready, w_ready, selb_ready = (
            sem(n) for n in ("lt_done", "lsh_ready", "lex_ready", "w_ready", "selb_ready"))
        rdve, ld_c, rfill, w_stored, dc_done, dc_read, cnt_done, nt_ready, tb_done, e_ready, tabs_done, tabs_ready = (
            sem(n) for n in ("rdve", "ld_c", "rfill", "w_stored", "dc_done", "dc_read", "cnt_done", "nt_ready",
                             "tb_done", "e_ready", "tabs_done", "tabs_ready"))
        steps_begun = sem("steps_begun")
        ztrash, trashed = sem("ztrash"), sem("trashed")
        ld_s = sem("ld_s")
        ld_e = sem("ld_e")
        sgu_done, ssil_ready, sact_ready, sd_done, so_ready = (
            sem(n) for n in ("sgu_done", "ssil_ready", "sact_ready", "sd_done", "so_ready"))
        step_ready, i_done, cmp_ready, idx_ready, sidx_ready, xa_done, xa_ready, gu_done, sil_ready, act_ready, dn_done, y_ready = (
            sem(n) for n in ("step_ready", "i_done", "cmp_ready", "idx_ready", "sidx_ready", "xa_done", "xa_ready", "gu_done",
                             "sil_ready", "act_ready", "dn_done", "y_ready"))
        hx_loaded = [sem(f"hx_loaded{i}") for i in range(8)]
        added = [sem(f"added{i}") for i in range(2)]
        ld_f = [[sem(f"ld_f{a}_{i}") for i in range(8)] for a in range(2)]
        f_ready, f_stored = sem("f_ready"), sem("f_stored")

        STEPS, HEAD, TAIL = TILES + 3, 4, 3
        NLW, NLO, NLM = 3, 4, 10

        def live(s, off):
            return 0 <= s - off < TILES

        XSTEPS, XUNROLL, XHEAD, XTAIL = SLOT_TILES + 9, 32, 32, 9
        EARLY = TILES - SLOT_TILES // 8
        FCH = 8
        FR = TILES // FCH

        def shared_now(v, s):
            u = s % 8
            return (v - u + 8 * EARLY, u) if s - u < SLOT_TILES else (None, None)

        def phase_a_over(eng):
            eng.wait_ge(g_ready, TILES)
            eng.wait_ge(hT_kept, TILES)
            for b in range(2):
                eng.wait_ge(x1_stored[b], 16 * TILES // 2)
                eng.wait_ge(h_stored[b], 16 * TILES // 2)

        def alive(s, off):
            return 0 <= s - off < SLOT_TILES

        def experts_window(eng, v, s):
            window = ()
            for at, n, there in ((v - 8, 8, s >= 8), (v, XUNROLL, s < SLOT_TILES)):
                if there:
                    _, values = nc.values_load_multi_w_load_instructions(
                        e_tab[0:1, bass.ds(at, n)], engines=[eng.engine], min_val=0, max_val=NX - 1,
                        skip_runtime_bounds_check_because="a one-hot over the experts makes them")
                    window += tuple(values)
                else:
                    window += (None,) * n
            return window

        block = ctx.enter_context(nc.Block())

        @block.sync
        def _(sp):
            sp.dma_start(subj_sb[:, :], subj).then_inc(ld_idx, 16)
            xv = x.rearrange("(i p) e -> p i e", p=P)
            for b in range(XB):
                sp.dma_start(xr[:, b, :], xv[:, b, :]).then_inc(ld_x[b], 16)
            for w, d in ((wk_sb, wk), (wq_sb, wq), (wv_sb, wv)):
                sp.dma_start(w[:, :, :], d.rearrange("(c p) n -> p c n", p=P)).then_inc(ld_w, 16)

            sp.wait_ge(put_w, 16)
            sp.dma_start(wrow[:, :, :], wsel_dram.rearrange("(i j) (c d) -> (j c) i d", j=NB, c=S)).then_inc(ld_wrow, 16)
            sp.wait_ge(put_b, 16)
            bias_by_token = bsel_dram.rearrange("b s -> (b s)")
            for b in range(XB):
                sp.dma_start(cb[:, b, :], bias_by_token[b * P:(b + 1) * P].partition_broadcast(P)).then_inc(ld_cb[b], 16)
            for w, d in ((wo_sb, wo), (w2_sb, w2), (at_sb, at)):
                sp.dma_start(w[:, :, :], d.rearrange("(c p) n -> p c n", p=P)).then_inc(ld_o, 16)
            sp.dma_start(bm_sb[:, :], bm).then_inc(ld_o, 16)
            sp.wait_ge(ztrash, 1)
            sp.dma_start(htab[T:ROWS, :], zrow[:, :]).then_inc(trashed, 16)
            for a_ in acc:
                sp.dma_start(a_[T:ROWS, :], zrow[:, 0:E]).then_inc(trashed, 16)
            assert NX == TILES

            def stores(v, s):
                if live(s, 0):
                    sp.dma_start(wgu_sb[:, :, bass.ds(v, 1), :], wgu.rearrange("(c p) e n -> p c e n", p=P)[:, :, bass.ds(v, 1), :]).then_inc(ld_e, 16)
                    sp.dma_start(wd_sb[:, bass.ds(v, 1), :], wd.rearrange("e p n -> p e n")[:, bass.ds(v, 1), :]).then_inc(ld_e, 16)
                    sp.dma_start(acc[1][bass.ds(v * P, P), :], zrow[:, 0:E]).then_inc(trashed, 16)
                if s == XB - 1:
                    for w_, d_ in ((sg_sb, sg), (su_sb, su), (sd_sb, sd)):
                        sp.dma_start(w_[:, :, :], d_.rearrange("(c p) n -> p c n", p=P)).then_inc(ld_s, 16)
                if live(s, 2):
                    t, b = v - 2, (s - 2) % 2
                    sp.wait_ge(x1_ready, t + 1)
                    sp.dma_start(acc[0][bass.ds(t * P, P), :], x1[:, b, :]).then_inc(x1_stored[b], 16)
                    if live(s, 2 - XB):
                        n = (s - 2) % XB
                        sp.dma_start(xr[:, n, :], x[bass.ds((t + XB) * P, P), :]).then_inc(ld_x[n], 16)
                        sp.dma_start(cb[:, n, :], bias_by_token[bass.ds((t + XB) * P, P)].partition_broadcast(P)).then_inc(ld_cb[n], 16)
                if live(s, 2):
                    t, b = v - 2, (s - 2) % 2
                    sp.wait_ge(h_ready, t + 1)
                    sp.dma_start(htab[bass.ds(t * P, P), 0:E], hrow[:, b, :]).then_inc(h_stored[b], 16)
            run_steps(sp, STEPS, HEAD, TAIL + XB, XB, stores)
            phase_a_over(sp)
            for t_, d_ in ((tri_sb, tri), (tail2_sb, tail2), (tailr_sb, tailr), (io_sb, iotas), (ec_sb, ecols),
                           (pcol_sb, pcol)):
                sp.dma_start(t_[tuple(slice(None) for _ in t_.shape)], d_).then_inc(ld_c, 16)

            def store_weights():
                sp.wait_ge(w_ready, 1)
                sp.dma_start(htab[0:T, E:HXW].rearrange("(i p) e -> p i e", p=P), rt[:, :, :]).then_inc(w_stored, 16)

            store_weights()

            rows = [a_[0:T, :].rearrange("(i p) e -> p i e", p=P) for a_ in (*acc, out)]
            for a_, f_ in enumerate((fa, fb)):
                sp.wait_ge(added[a_], 16 * SLOT_TILES // 2)
                for k in range(FCH):
                    i_ = slice(k * FR, (k + 1) * FR)
                    sp.dma_start(f_[:, i_, :], rows[a_][:, i_, :]).then_inc(ld_f[a_][k], 16)
            for k in range(FCH):
                i_ = slice(k * FR, (k + 1) * FR)
                sp.wait_ge(f_ready, FCH + k + 1)
                sp.dma_start(rows[2][:, i_, :], fa[:, i_, :]).then_inc(f_stored, 16)
            sp.wait_ge(f_stored, 16 * FCH)

        @block.gpsimd
        def _(pool):
            pool.wait_ge(ld_idx, 16)
            pool.indirect_dma_start(wsel[:, :], None, wcond, bass.IndirectOffsetOnAxis(subj_sb[:, 0:1], 0)).then_inc(got_w, 16)
            pool.indirect_dma_start(bsel[:, :], None, fside, bass.IndirectOffsetOnAxis(subj_sb[:, 0:1], 0)).then_inc(got_b, 16)
            pool.memset(vp[:, :, :, :, :, :], 0.0).then_inc(zeroed, 1)
            pool.memset(pbd[:, :, :], 0.0).then_inc(zeroed, 1)
            pool.memset(zrow[:, :], 0.0).then_inc(ztrash, 1)
            pool.wait_ge(ld_q, 32)
            pool.wait_ge(ld_wrow, 16)

            def make_wbd(t, n):
                pool.tensor_tensor(wbd[:, n, :, :], wrow[:, bass.ds(t, 1), :].broadcast_to([P, NB, S]),
                                   qmask_sb[:, :, None].broadcast_to([P, NB, S]), ALU.mult).then_inc(wbd_ready, 1)
            make_wbd(0, 0)

            def steps(v, s):
                if live(s, 0):
                    t = v
                    pool.wait_ge(c_done, t + 1)
                    if s == 0:
                        pool.wait_ge(ld_m, 16 * NLM)
                    pool.tensor_tensor(xr[:, s % XB, :], xr[:, s % XB, :], bo_sb[:, :], ALU.add).then_inc(xbo_ready, 1)
                    if live(s, -1):
                        make_wbd(t + 1, (s + 1) % 2)
                if live(s, 0):
                    t = v
                    for c in range(KC):
                        if c == 0 and s >= 1:
                            pool.wait_ge(s_done, t)
                        pool.wait_ge(k_ready, KC * t + c + 1)
                        pool.tensor_tensor(
                            kbd[:, c, :, :, :],
                            kT[:, c, :].rearrange("p (j k) -> p j k", j=NB)[:, :, None, :].broadcast_to([P, NB, HC, S]),
                            hmask_sb[:, None, :, None].broadcast_to([P, NB, HC, S]), ALU.mult).then_inc(kbd_ready, 1)
                if live(s, 3):
                    t = v - 3
                    pool.wait_ge(hT_ready, t + 1)
                    pool.tensor_copy(hT[:, bass.ds(t, 1), :, :], hTs[:, (s - 3) % 2, None, :, :]).then_inc(hT_kept, 1)
            run_steps(pool, STEPS, HEAD, TAIL + XB, XB, steps)

            phase_a_over(pool)
            pool.memset(gs[:, :, :], -1.0).then_inc(rfill, 1)
            pool.memset(ts[:, :, :], -1.0).then_inc(rfill, 1)
            pool.memset(selb[:, :, :], 0.0).then_inc(rfill, 1)
            pool.memset(one_b[:, :], 1.0).then_inc(rfill, 1)


            def experts_dma(v, s):
                if alive(s, 1):
                    t = v - 1
                    pool.wait_ge(idx_ready, t + 1)
                    if s - 1 >= 8:
                        pool.wait_ge(act_ready, t - 7)
                        pool.wait_ge(xa_done, t - 7)
                if alive(s, 9):
                    t, p_ = v - 9, (s - 9) % 2
                    pool.wait_ge(y_ready, t + 1)
                    pool.wait_ge(sidx_ready, t + 1)
                    if s - 9 >= 2:
                        pool.wait_ge(added[p_], (t - p_) * 8)
                pool.sem_inc(steps_begun, 1)
                if alive(s, 9):
                    t, p_ = v - 9, (s - 9) % 2
                    pool.wait_ge(trashed, 48 + 16 * TILES)
                    pool.indirect_dma_start(acc[p_], bass.IndirectOffsetOnAxis(sidx[:, (s - 9) % 8:(s - 9) % 8 + 1], 0),
                                            y[:, (s - 9) % 4, :], None, compute_op=ALU.add).then_inc(added[p_], 16)
                if alive(s, 1):
                    pool.wait_ge(w_stored, 16)
                    pool.indirect_dma_start(hx[:, (s - 1) % 8, :], None, htab,
                                            bass.IndirectOffsetOnAxis(idx[:, (s - 1) % 8:(s - 1) % 8 + 1], 0)).then_inc(hx_loaded[(s - 1) % 8], 16)
            run_steps(pool, XSTEPS, XHEAD, XTAIL, XUNROLL, experts_dma)

        @block.scalar
        def _(act):
            act.dma_start(qmask_sb[:, :], quadmask).then_inc(ld_q, 16)
            act.dma_start(hmask_sb[:, :], headmask).then_inc(ld_q, 16)
            act.wait_ge(got_w, 16)
            act.dma_start(wsel_dram, wsel[:, :]).then_inc(put_w, 16)
            act.wait_ge(got_b, 16)
            act.dma_start(bsel_dram, bsel[:, :]).then_inc(put_b, 16)
            for t_, d in ((bq_sb, bq), (bk_sb, bk), (bv_sb, bv)):
                act.dma_start(t_[:, :], d).then_inc(ld_m, 16)
            act.dma_start(bo_sb[:, :], bo.partition_broadcast(P)).then_inc(ld_m, 16)
            act.dma_start(alibi_sb[:, :, :], alibi).then_inc(ld_m, 16)
            act.dma_start(adp_i[:, :], adapter.partition_broadcast(P)).then_inc(ld_m, 16)
            act.dma_start(scal_sb[:, :], scal).then_inc(ld_m, 16)
            act.dma_start(acol_sb[:, :], acol).then_inc(ld_m, 16)
            act.dma_start(id_sb[:, :], ident).then_inc(ld_m, 16)
            act.dma_start(wg_sb[:, :, :], wg.rearrange("(c p) n -> p c n", p=P)).then_inc(ld_m, 16)
            act.wait_ge(ld_m, 16 * NLM)
            act.wait_ge(zeroed, 2)

            def steps(v, s):
                if live(s, 2):
                    t = v - 2
                    act.wait_ge(o_done, t + 1)
                    if s - 2 >= 1:
                        act.wait_ge(w_done, t)
                    for c in range(KC):
                        ins = act.activation(oT[:, c, :], ps_o[:, c * P:(c + 1) * P], ACT.Identity, bias=bv_sb[:, c:c + 1])
                    ins.then_inc(oT_ready, 1)
                if live(s, 1):
                    t = v - 1
                    act.wait_ge(sh_ready, t + 1)
                    if s - 1 >= 1:
                        act.wait_ge(pr_ready, t)
                    act.activation(ex[:, :, :], sh[:, :, :], ACT.Exp).then_inc(ex_ready, 1)
                if live(s, 3):
                    t = v - 3
                    act.wait_ge(ht_done, t + 1)
                    if s - 3 >= 2:
                        act.wait_ge(g_done, t - 1)
                        act.wait_ge(hT_kept, t - 1)
                    act.activation(hTs[:, (s - 3) % 2, :, :], ps_t[:, :, :], ACT.Copy).then_inc(hT_ready, 1)
                if live(s, 0):
                    t = v
                    act.wait_ge(k_done, t + 1)
                    if s >= 1:
                        act.wait_ge(kbd_ready, 2 * t)
                    for c in range(KC):
                        act.activation(kT[:, c, :], ps_k[:, c, :], ACT.Identity, bias=bk_sb[:, c:c + 1]).then_inc(k_ready, 1)
                    act.wait_ge(q_done, t + 1)
                    if s >= 1:
                        act.wait_ge(s_done, t)
                    for c in range(KC):
                        ins = act.activation(qT[:, c, :], ps_q[:, c, :], ACT.Identity, bias=bq_sb[:, c:c + 1])
                    ins.then_inc(q_ready, 1)
                if live(s, 2):
                    t = v - 2
                    act.wait_ge(x1t_done, t + 1)
                    if s - 2 >= 1:
                        act.wait_ge(h_done, t)
                    act.activation(x1T[:, :, :], ps_t[:, :, :], ACT.Copy).then_inc(x1T_ready, 1)
                if live(s, 0):
                    t = v
                    act.wait_ge(v_done, t + 1)
                    if s >= 2:
                        act.wait_ge(o_done, t - 1)
                    for a in range(2):
                        ins = act.activation(vp[:, s % 2, :, a, a, :], ps_cv[:, :, :].rearrange("p c (n a d) -> p (c n) a d", a=2, d=D)[:, :, a, :], ACT.Copy)
                    ins.then_inc(v_ready, 1)
                if live(s, 3):
                    t, q = v - 3, (s - 3) % 4
                    act.wait_ge(g_done, t + 1)
                    act.activation(lgT[q * 32:(q + 1) * 32, bass.ds((t - q) * 32, P)], ps_o[q * 32:(q + 1) * 32, 0:P], ACT.Copy).then_inc(g_ready, 1)
                if live(s, 2):
                    t, b = v - 2, (s - 2) % 2
                    act.wait_ge(h_done, t + 1)
                    if s - 2 >= 2:
                        act.wait_ge(h_stored[b], (t - b) * 8)
                        act.wait_ge(ht_done, t - 1)
                    act.activation(hrow[:, b, :], ps_w[:, :], ACT.Copy).then_inc(h_ready, 1)
            run_steps(act, STEPS, HEAD, TAIL, XB, steps)

            phase_a_over(act)
            act.wait_ge(lsh_ready, 2)
            act.activation(rt[:, :, :], rt[:, :, :], ACT.Exp).then_inc(lex_ready, 1)

            def shared_silu(n8, ps=ps_sh):
                act.wait_ge(sgu_done, n8 + 8)
                if not isinstance(n8, int) or n8 > 0:
                    act.wait_ge(sact_ready, n8)
                act.activation(ssil[:, :], ps[:, 0:FC * P], ACT.Silu).then_inc(ssil_ready, 8)

            def shared_out(n8, ps=ps_sh):
                act.wait_ge(sd_done, n8 + 8)
                act.activation(h_flat[:, bass.ds(n8 * (E // 8), E)], ps[:, 0:E], ACT.Copy).then_inc(so_ready, 8)

            for n in range(EARLY):
                shared_silu(8 * n, early_banks[n])
                if n >= 1:
                    shared_out(8 * (n - 1), early_banks[n - 1])
            shared_out(8 * (EARLY - 1), early_banks[EARLY - 1])
            for n in range(NDC):
                e_ = range(3 * n, min(3 * n + 3, NX))
                act.wait_ge(dc_done, n + 1)
                act.activation(dc[:, e_[0]:e_[-1] + 1, :], ps_r[n % 4][0:NI, 0:len(e_) * DCW].rearrange("p (e n) -> p e n", n=DCW), ACT.Copy).then_inc(dc_read, 1)

            def experts_act(v, s):
                if alive(s, 4) or alive(s, 7):
                    b = (s - 4) % 2
                    part = slice(0 if alive(s, 4) else E, E + F if alive(s, 7) else E)
                    act.wait_ge(xa_done, v - 3)
                    if alive(s, 6):
                        act.wait_ge(gu_done, v - 5)
                    if alive(s, 9):
                        act.wait_ge(dn_done, v - 8)
                    act.activation(xa[:, b, part], ps_x[b][:, part], ACT.Copy).then_inc(xa_ready, 1)
                if alive(s, 5):
                    t, b = v - 5, (s - 5) % 2
                    act.wait_ge(gu_done, t + 1)
                    if s - 5 >= 2:
                        act.wait_ge(act_ready, t - 1)
                    act.activation(sil[:, b, :], ps_gu[b][:, 0:F], ACT.Silu).then_inc(sil_ready, 1)
                if alive(s, 8):
                    t = v - 8
                    act.wait_ge(dn_done, t + 1)
                    if s - 8 >= 4:
                        p_ = (s - 8) % 2
                        act.wait_ge(added[p_], (t - p_ - 2) * 8)
                    act.activation(y[:, (s - 8) % 4, :], ps_y[(s - 8) % 2][:, 0:E], ACT.Copy).then_inc(y_ready, 1)
                n8, stage = shared_now(v, s)
                if stage == 4:
                    shared_silu(n8)
                if stage == 7:
                    shared_out(n8)
            run_steps(act, XSTEPS, XHEAD, XTAIL, XUNROLL, experts_act)

        @block.vector
        def _(dve):
            dve.wait_ge(ld_m, 16 * NLM)
            dve.tensor_copy(adp_f[:, :], adp_i[:, :]).then_inc(adp_ready, 1)
            dve.wait_ge(adp_ready, 1)
            dve.tensor_scalar(lmask[:, :], adp_f[:, :], acol_sb[:, 0:1], scal_sb[:, 0:1], ALU.is_equal, ALU.mult).then_inc(lmask_ready, 1)
            dve.wait_ge(lmask_ready, 1)

            def steps(v, s):
                if live(s, 1):
                    t = v - 1
                    dve.wait_ge(s_done, t + 1)
                    dve.scalar_tensor_tensor(sc[:, :, :].rearrange("p h k -> p (h k)"), ps_s[:, :], float(D) ** -0.5,
                                             alibi_sb[:, :, :].rearrange("p h k -> p (h k)"), ALU.mult, ALU.add).then_inc(sc_ready, 1)
                    dve.wait_ge(sc_ready, t + 1)
                    dve.tensor_reduce(mx[:, :], sc[:, :, :], AX, ALU.max).then_inc(mx_ready, 1)
                    dve.wait_ge(mx_ready, t + 1)
                    if s - 1 >= 1:
                        dve.wait_ge(ex_ready, t)
                    dve.tensor_tensor(sh[:, :, :], sc[:, :, :], mx[:, :, None].broadcast_to([P, H, S]), ALU.subtract).then_inc(sh_ready, 1)
                if live(s, 0):
                    t = v
                    dve.wait_ge(c_done, t + 1)
                    if s >= 1:
                        dve.wait_ge(v_done, t)
                    dve.wait_ge(ld_cb[s % XB], (t - s % XB) * (16 // XB) + 16)
                    dve.tensor_tensor(cT[:, :, :], ps_cv[:, :, :],
                                      cb[:, s % XB, None, :].broadcast_to([P, KC, P]), ALU.add).then_inc(cT_ready, 1)
                if live(s, 1):
                    t = v - 1
                    dve.wait_ge(ex_ready, t + 1)
                    dve.tensor_reduce(sm[:, :], ex[:, :, :], AX, ALU.add).then_inc(sm_ready, 1)
                    dve.wait_ge(sm_ready, t + 1)
                    dve.reciprocal(rs[:, :], sm[:, :]).then_inc(rs_ready, 1)
                if live(s, 2):
                    t, b = v - 2, (s - 2) % 2
                    dve.wait_ge(w_done, t + 1)
                    dve.wait_ge(xbo_ready, t + 1)
                    if s - 2 >= 2:
                        dve.wait_ge(x1_stored[b], (t - b) * 8)
                        dve.wait_ge(x1t_done, t - 1)
                    dve.tensor_tensor(x1[:, b, :], ps_w[:, :], xr[:, (s - 2) % XB, :], ALU.add).then_inc(x1_ready, 1)
                if live(s, 1):
                    t = v - 1
                    dve.wait_ge(rs_ready, t + 1)
                    dve.tensor_tensor(pr[:, :, :], ex[:, :, :], rs[:, :, None].broadcast_to([P, H, S]), ALU.mult).then_inc(pr_ready, 1)
                    if s - 1 >= 1:
                        dve.wait_ge(o_done, t)
                    dve.wait_ge(pr_ready, t + 1)
                    if s == 1:
                        dve.wait_ge(zeroed, 2)
                    for j in range(NB - 1):
                        q = slice(j * S, (j + 1) * S)
                        dve.transpose(pbd[q, :, q], pr[q, :, :])
                if live(s, 2):
                    t = v - 2
                    dve.wait_ge(a_done, t + 1)
                    if s - 2 >= 1:
                        dve.wait_ge(h_done, t)
                    dve.tensor_tensor(xam[:, :].rearrange("p (j k) -> p j k", j=NB), ps_a[:, :].rearrange("p (j k) -> p j k", j=NB),
                                      lmask[:, bass.ds(t * NB, NB), None].broadcast_to([P, NB, S]), ALU.mult).then_inc(xam_ready, 1)
                if live(s, 1):
                    q = slice((NB - 1) * S, P)
                    dve.transpose(pbd[q, :, q], pr[q, :, :]).then_inc(pbd_ready, 1)
            run_steps(dve, STEPS, HEAD, TAIL, XB, steps)

            def shared_mult(n8, ps=ps_sh):
                dve.wait_ge(ssil_ready, n8 + 8)
                if not isinstance(n8, int) or n8 > 0:
                    dve.wait_ge(sd_done, n8)
                dve.tensor_tensor(sact[:, :], ssil[:, :], ps[:, FC * P:2 * FC * P], ALU.mult).then_inc(sact_ready, 8)

            assert EARLY == 4
            phase_a_over(dve)
            HT = TILES // 2
            for h_ in range(2):
                dve.wait_ge(lt_done, h_ + 1)
                dve.tensor_reduce(lmx[:, h_ * HT:(h_ + 1) * HT], ps_r[h_][:, :].rearrange("p (i e) -> p i e", e=NX), AX, ALU.max).then_inc(rdve, 1)
            for h_ in range(2):
                dve.wait_ge(rdve, h_ + 1)
                dve.tensor_tensor(rt[:, h_ * HT:(h_ + 1) * HT, :], ps_r[h_][:, :].rearrange("p (i e) -> p i e", e=NX),
                                  lmx[:, h_ * HT:(h_ + 1) * HT, None].broadcast_to([P, HT, NX]), ALU.subtract).then_inc(lsh_ready, 1)
            dve.wait_ge(lex_ready, 1)
            dve.tensor_reduce(lsum[:, :], rt[:, :, :], AX, ALU.add).then_inc(rdve, 1)
            dve.wait_ge(rdve, 3)
            dve.reciprocal(lrs[:, :], lsum[:, :]).then_inc(rdve, 1)
            dve.wait_ge(rdve, 4)
            dve.tensor_tensor(rt[:, :, :], rt[:, :, :], lrs[:, :, None].broadcast_to([P, TILES, NX]), ALU.mult).then_inc(rdve, 1)
            dve.wait_ge(rdve, 5)
            dve.wait_ge(rfill, 4)
            dve.tensor_reduce(gs[:, :, 0:G], rt[:, :, :].rearrange("p i (g k) -> p i g k", g=G), AX, ALU.max).then_inc(rdve, 1)
            dve.wait_ge(rdve, 6)
            for t in range(TILES):
                ins = dve.max(m8[:, t, :], gs[:, t, 0:G])
            ins.then_inc(rdve, 1)
            shared_mult(8 * 0, early_banks[0])
            dve.wait_ge(rdve, 7)
            dve.memset(m8[:, :, TOP_GROUPS:8], -1.0).then_inc(rdve, 1)
            dve.wait_ge(rdve, 8)
            for t in range(TILES):
                ins = dve.match_replace(gr[:, t, :], m8[:, t, :], gs[:, t, :], -2.0)
            ins.then_inc(rdve, 1)
            shared_mult(8 * 1, early_banks[1])
            dve.wait_ge(rdve, 9)
            dve.tensor_scalar(gmask[:, :, :], gr[:, :, 0:G], -2.0, None, ALU.is_equal).then_inc(rdve, 1)
            dve.wait_ge(rdve, 10)
            dve.tensor_tensor(ts[:, :, 0:NX].rearrange("p i (g k) -> p i g k", g=G), rt[:, :, :].rearrange("p i (g k) -> p i g k", g=G),
                              gmask[:, :, :, None].broadcast_to([P, TILES, G, NX // G]), ALU.mult).then_inc(rdve, 1)
            dve.wait_ge(rdve, 11)
            for t in range(TILES):
                ins = dve.max(e8[:, t, :], ts[:, t, 0:NX])
            ins.then_inc(rdve, 1)
            shared_mult(8 * 2, early_banks[2])
            dve.wait_ge(rdve, 12)
            dve.memset(e8[:, :, TOP_K:8], -1.0).then_inc(rdve, 1)
            dve.wait_ge(rdve, 13)
            for t in range(TILES):
                ins = dve.match_replace(tr[:, t, :], e8[:, t, :], ts[:, t, :], -2.0)
            ins.then_inc(rdve, 1)
            shared_mult(8 * 3, early_banks[3])
            dve.wait_ge(rdve, 14)
            dve.tensor_scalar(sel[:, :, :], tr[:, :, 0:NX], -2.0, None, ALU.is_equal).then_inc(rdve, 1)
            dve.wait_ge(rdve, 15)
            dve.tensor_copy(selb[:, :, 1:TILES + 1], sel[:, :, :].rearrange("p i e -> p e i")).then_inc(selb_ready, 1)
            dve.tensor_tensor(rt[:, :, :], ts[:, :, 0:NX], sel[:, :, :], ALU.mult).then_inc(rdve, 1)
            dve.wait_ge(rdve, 16)
            dve.tensor_reduce(wsum[:, :], rt[:, :, :], AX, ALU.add).then_inc(rdve, 1)
            dve.wait_ge(cnt_done, 1)
            dve.wait_ge(ld_c, 96)
            dve.memset(pre[:, 0:1], 0.0).then_inc(rdve, 1)
            dve.tensor_tensor_scan(pre[:, 1:NI], ec_sb[0:NX, 2 * NX:3 * NX], ps_y[0][0:NX, 0:TILES], 0.0, ALU.mult, ALU.add).then_inc(rdve, 1)
            dve.wait_ge(rdve, 19)
            dve.tensor_scalar(nti[:, 0:1], pre[:, TILES:NI], float(P - 1), None, ALU.add).then_inc(rdve, 1)
            dve.wait_ge(rdve, 20)
            dve.tensor_scalar(nti[:, 1:2], nti[:, 0:1], 7, None, ALU.arith_shift_right).then_inc(rdve, 1)
            dve.wait_ge(rdve, 21)
            dve.tensor_copy(ntf[:, 0:1], nti[:, 1:2]).then_inc(nt_ready, 1)
            dve.wait_ge(rdve, 17)
            dve.tensor_scalar(wsum[:, :], wsum[:, :], 1e-20, None, ALU.add).then_inc(rdve, 1)
            dve.wait_ge(rdve, 22)
            dve.reciprocal(wrs[:, :], wsum[:, :]).then_inc(rdve, 1)
            dve.wait_ge(rdve, 23)
            dve.tensor_tensor(rt[:, :, :], rt[:, :, :], wrs[:, :, None].broadcast_to([P, TILES, NX]), ALU.mult).then_inc(w_ready, 1)

            dve.wait_ge(tb_done, 1)
            dve.tensor_copy(ntf[:, 1:2], ps_y[1][0:NX, 0:1]).then_inc(rdve, 1)
            dve.wait_ge(rdve, 24)
            dve.wait_ge(nt_ready, 1)
            dve.scalar_tensor_tensor(ntf[:, 2:3], ntf[:, 0:1], ntf[:, 1:2], ec_sb[:, 4 * NX + 1:4 * NX + 2], ALU.add, ALU.add).then_inc(rdve, 1)
            dve.tensor_scalar(ntf[:, 3:4], ntf[:, 1:2], float(P), None, ALU.mult).then_inc(rdve, 1)
            dve.tensor_scalar(e1[:, :], io_sb[0:NX, 0, :], ntf[:, 1:2], None, ALU.is_ge).then_inc(rdve, 1)
            dve.wait_ge(rdve, 27)
            dve.scalar_tensor_tensor(e2[:, :], io_sb[0:NX, 0, :], ntf[:, 2:3], e1[:, :], ALU.is_lt, ALU.mult).then_inc(e_ready, 1)
            dve.tensor_scalar(r0e[:, :], io_sb[0:NX, 1, :], ntf[:, 3:4], pre[:, TILES:NI], ALU.subtract, ALU.min).then_inc(rdve, 1)
            dve.wait_ge(rdve, 28)
            dve.wait_ge(e_ready, 1)
            dve.tensor_tensor(ea[:, :], r0e[:, :], e2[:, :], ALU.mult).then_inc(e_ready, 1)
            dve.wait_ge(tabs_done, 1)
            steps_ps, rank_ps = ps_y
            dve.tensor_copy(pr_tab[:, :], steps_ps[0:NI, 0:SLOT_TILES]).then_inc(tabs_ready, 1)
            dve.tensor_copy(e_tab[:, :], steps_ps[0:1, 256:256 + SLOT_TILES]).then_inc(tabs_ready, 1)
            dve.tensor_scalar(r0_tab[:, :], rank_ps[:, 0:SLOT_TILES], pcol_sb[:, 0:1], None, ALU.add).then_inc(tabs_ready, 1)
            dve.tensor_copy(iop[:, :], io_sb[0:NI, 0, 0:P]).then_inc(tabs_ready, 1)
            dve.wait_ge(tabs_ready, 4)
            dve.wait_ge(w_stored, 16)
            regs = {}

            def experts_of(v, s):
                regs["e"] = experts_window(dve, v, s)

            def expert(s, off):
                return regs["e"][8 + s % XUNROLL - off]

            def experts_dve(v, s):
                if alive(s, 0):
                    t = v
                    if s >= 2:
                        dve.wait_ge(i_done, t - 1)
                    dve.tensor_scalar(step_sb[:, s % 2, :], iop[:, :], pr_tab[:, bass.ds(t, 1)], None, ALU.is_ge).then_inc(step_ready, 1)
                if alive(s, 5):
                    t, b = v - 5, (s - 5) % 2
                    dve.wait_ge(sil_ready, t + 1)
                    if s - 5 >= 4:
                        dve.wait_ge(xa_done, v - 5)
                    dve.scalar_tensor_tensor(act_x[:, (s - 5) % 4, :], sil[:, b, :], hx[:, (s - 5) % 8, bass.ds(expert(s, 5) + E, 1)],
                                             ps_gu[b][:, F:2 * F], ALU.mult, ALU.mult).then_inc(act_ready, 1)
                if alive(s, 0):
                    t = v
                    dve.wait_ge(i_done, t + 1)
                    if s >= 1:
                        dve.wait_ge(idx_ready, t)
                    dve.tensor_scalar(cmp[:, :], ps_i[:, 0:P], r0_tab[:, bass.ds(t, 1)], 0.0, ALU.is_le, ALU.add,
                                      accum_out=cnt[:, s % 2:s % 2 + 1]).then_inc(cmp_ready, 1)
                    dve.wait_ge(cmp_ready, t + 1)
                    if s >= 8:
                        dve.wait_ge(hx_loaded[s % 8], (t - s % 8) * 2)
                        dve.wait_ge(sidx_ready, t - 7)
                    dve.tensor_tensor(idx[:, s % 8:s % 8 + 1], ps_i[:, P:P + 1], cnt[:, s % 2:s % 2 + 1], ALU.add).then_inc(idx_ready, 1)
                if alive(s, 5):
                    t = v - 5
                    if s - 5 >= 8:
                        dve.wait_ge(added[(s - 5) % 2], (t - (s - 5) % 2) * 8 - 48)
                    dve.wait_ge(idx_ready, t + 1)
                    dve.tensor_copy(sidx[:, (s - 5) % 8:(s - 5) % 8 + 1], idx[:, (s - 5) % 8:(s - 5) % 8 + 1]).then_inc(sidx_ready, 1)
                n8, stage = shared_now(v, s)
                if stage == 4:
                    shared_mult(n8)
            run_steps(dve, XSTEPS, XHEAD, XTAIL, XUNROLL, experts_dve, experts_of)

            dve.wait_ge(so_ready, 8 * TILES)
            for a_, f_ in enumerate((h_flat.rearrange("p (i e) -> p i e", e=E), fb)):
                for k in range(FCH):
                    i_ = slice(k * FR, (k + 1) * FR)
                    dve.wait_ge(ld_f[a_][k], 16)
                    if a_ == 1:
                        dve.wait_ge(f_ready, k + 1)
                    dve.tensor_tensor(fa[:, i_, :], fa[:, i_, :], f_[:, i_, :], ALU.add).then_inc(f_ready, 1)

        @block.tensor
        def _(pe):
            pe.wait_ge(ld_w, 16 * NLW)

            def steps(v, s):
                if live(s, 1):
                    t = v - 1
                    if s - 1 >= 1:
                        pe.wait_ge(sc_ready, t)
                    pe.wait_ge(q_ready, t + 1)
                    for c in range(KC):
                        pe.wait_ge(kbd_ready, 2 * t + 1 + c)
                        for j in range(NB):
                            ins = pe.matmul(ps_s[j * S:(j + 1) * S, c * HC * S:(c + 1) * HC * S], qT[:, c, j * S:(j + 1) * S],
                                            kbd[:, c, j, :, :].rearrange("p h k -> p (h k)"), start=True, stop=True)
                    ins.then_inc(s_done, 1)
                if live(s, 2):
                    t, b = v - 2, (s - 2) % 2
                    if s - 2 >= 2:
                        pe.wait_ge(g_ready, t - 1)
                    pe.wait_ge(pbd_ready, t + 1)
                    pe.wait_ge(v_ready, t + 1)
                    for c in range(KC):
                        for a in range(2):
                            for g in range(NB):
                                pair = c * NB + g
                                ins = pe.matmul(ps_o[g * S:(g + 1) * S, c * P:(c + 1) * P], vp[:, b, pair, a, :, :].rearrange("p a d -> p (a d)"),
                                                pbd[:, 2 * pair + a, :], start=(a == 0), stop=(a == 1))
                    ins.then_inc(o_done, 1)
                if live(s, 0):
                    t = v
                    if s >= 1:
                        pe.wait_ge(v_ready, t)
                    pe.wait_ge(wbd_ready, t + 1)
                    pe.wait_ge(ld_x[s % XB], (t - s % XB) * (16 // XB) + 16)
                    for c in range(KC):
                        ins = pe.matmul(ps_cv[:, c, :], xr[:, s % XB, c * P:(c + 1) * P], wbd[:, s % 2, :, :].rearrange("p j d -> p (j d)"), start=True, stop=True)
                    ins.then_inc(c_done, 1)
                if s == 2:
                    pe.wait_ge(ld_o, 16 * NLO)
                    pe.wait_ge(ld_m, 16 * NLM)
                if live(s, 3):
                    t, b = v - 3, (s - 3) % 2
                    pe.wait_ge(h_ready, t + 1)
                    pe.wait_ge(x1T_ready, t + 1)
                    for c in range(KC):
                        ins = pe.transpose(ps_t[:, c, :], hrow[:, b, c * P:(c + 1) * P], id_sb[:, :])
                    ins.then_inc(ht_done, 1)
                if live(s, 2):
                    t = v - 2
                    if s - 2 >= 1:
                        pe.wait_ge(h_ready, t)
                    pe.wait_ge(oT_ready, t + 1)
                    for c in range(KC):
                        ins = pe.matmul(ps_w[:, :], oT[:, c, :], wo_sb[:, c, :], start=(c == 0), stop=(c == KC - 1))
                    ins.then_inc(w_done, 1)
                if live(s, 0):
                    t = v
                    if s >= 1:
                        pe.wait_ge(q_ready, t)
                    pe.wait_ge(cT_ready, t + 1)
                    for w, ps, done in ((wk_sb, ps_k, k_done), (wq_sb, ps_q, q_done)):
                        for m in range(KC):
                            for c in range(KC):
                                ins = pe.matmul(ps[:, m, :], w[:, c, m * P:(m + 1) * P], cT[:, c, :], start=(c == 0), stop=(c == KC - 1))
                        ins.then_inc(done, 1)
                if live(s, 2):
                    t, b = v - 2, (s - 2) % 2
                    pe.wait_ge(x1_ready, t + 1)
                    if s - 2 >= 1:
                        pe.wait_ge(hT_ready, t)
                    for c in range(KC):
                        ins = pe.transpose(ps_t[:, c, :], x1[:, b, c * P:(c + 1) * P], id_sb[:, :])
                    ins.then_inc(x1t_done, 1)
                if live(s, 0):
                    for c in range(KC):
                        ins = pe.matmul(ps_cv[:, :, :].rearrange("p c n -> p (c n)"), cT[:, c, :], wv_sb[:, c, :], start=(c == 0), stop=(c == KC - 1))
                    ins.then_inc(v_done, 1)
                if live(s, 3):
                    t, q = v - 3, (s - 3) % 4
                    if s - 3 < TILES - 1:
                        pe.wait_ge(oT_ready, t + 2)
                    pe.wait_ge(hT_ready, t + 1)
                    for c in range(KC):
                        ins = pe.matmul(ps_o[q * 32:(q + 1) * 32, 0:P], wg_sb[:, c, :], hTs[:, (s - 3) % 2, c, :], start=(c == 0), stop=(c == KC - 1))
                    ins.then_inc(g_done, 1)
                if live(s, 2):
                    t = v - 2
                    if s - 2 >= 1:
                        pe.wait_ge(xam_ready, t)
                    pe.wait_ge(x1T_ready, t + 1)
                    for c in range(KC):
                        ins = pe.matmul(ps_a[:, :], at_sb[:, c, :], x1T[:, c, :], start=(c == 0), stop=(c == KC - 1))
                    ins.then_inc(a_done, 1)
                    for c in range(KC):
                        pe.matmul(ps_w[:, :], x1T[:, c, :], w2_sb[:, c, :], start=(c == 0), stop=False)
                    pe.wait_ge(xam_ready, t + 1)
                    pe.matmul(ps_w[:, :], xam[:, :], bm_sb[:, :], start=False, stop=True).then_inc(h_done, 1)
            run_steps(pe, STEPS, HEAD, TAIL, XB, steps)

            phase_a_over(pe)
            for a_ in range(TILES // 4):
                ins = pe.transpose(ps_r[a_ // 4][:, (a_ % 4) * P:(a_ % 4 + 1) * P], lgT[:, a_ * P:(a_ + 1) * P], id_sb[:, :])
                if a_ % 4 == 3:
                    ins.then_inc(lt_done, 1)
            pe.wait_ge(ld_s, 48)

            def shared_gate_up(n8, parts, ps=ps_sh):
                if 0 in parts and ps is ps_sh and (not isinstance(n8, int) or n8 > 0):
                    pe.wait_ge(so_ready, n8)
                for part in parts:
                    w_, m = (sg_sb, su_sb)[part // FC], part % FC
                    for c in range(KC):
                        ins = pe.matmul(ps[:, part * P:(part + 1) * P], w_[:, c, m * P:(m + 1) * P],
                                        h_flat[:, bass.ds(n8 * (E // 8) + c * P, P)], start=(c == 0), stop=(c == KC - 1))
                if 3 in parts:
                    ins.then_inc(sgu_done, 8)

            def shared_down(n8, parts, ps=ps_sh):
                pe.wait_ge(sact_ready, n8 + 8)
                for m in parts:
                    ins = pe.matmul(ps[:, 0:E], sact[:, m * P:(m + 1) * P], sd_sb[:, m, :], start=(m == 0), stop=(m == FC - 1))
                if FC - 1 in parts:
                    ins.then_inc(sd_done, 8)

            def choices():
                pe.wait_ge(selb_ready, 1)
                pe.wait_ge(ld_c, 96)
                pe.wait_ge(so_ready, 8 * EARLY)
                for t in range(TILES):
                    ins = pe.matmul(ps_y[0][0:NX, t:t + 1], selb[:, :, t + 1], one_b[:, 0:1], start=True, stop=True)
                ins.then_inc(cnt_done, 1)

            def increments(groups):
                for n in groups:
                    if n >= 4:
                        pe.wait_ge(dc_read, n - 3)
                    for k, e_ in enumerate(range(3 * n, min(3 * n + 3, NX))):
                        o_ = ps_r[n % 4][0:NI, k * DCW:(k + 1) * DCW]
                        pe.matmul(o_, selb[:, e_, 1:NI + 1], tri_sb[:, 0, :], start=True, stop=False)
                        pe.matmul(o_, selb[:, e_, 0:NI], tri_sb[:, 1, :], start=False, stop=False)
                        ins = pe.matmul(o_, tail2_sb[:, :], tailr_sb[:, :], start=False, stop=True)
                    ins.then_inc(dc_done, 1)

            def first_tiles():
                pe.wait_ge(nt_ready, 1)
                pe.matmul(ps_y[1][0:NX, 0:1], ec_sb[0:NX, 0:NX], ntf[:, 0:1], start=True, stop=True).then_inc(tb_done, 1)

            def slot_tables():
                pe.wait_ge(e_ready, 2)
                steps_ps, rank_ps = ps_y
                pe.matmul(steps_ps[0:NI, 0:SLOT_TILES], pre[:, :], e2[:, :], start=True, stop=False)
                pe.matmul(steps_ps[0:NI, 0:SLOT_TILES], ec_sb[0:NX, 3 * NX:4 * NX + 1][:, 0:NI], ea[:, :], start=False, stop=True)
                pe.matmul(steps_ps[0:NX, 256:256 + SLOT_TILES], ec_sb[0:NX, NX:2 * NX], e2[:, :], start=True, stop=True)
                for q in range(4):
                    ins = pe.matmul(rank_ps[q * 32:(q + 1) * 32, 0:SLOT_TILES], ec_sb[0:NX, 2 * NX:3 * NX], ea[:, :], start=True, stop=True)
                ins.then_inc(tabs_done, 1)

            for n in range(EARLY):
                shared_gate_up(8 * n, range(4), early_banks[n])
            for n in range(EARLY):
                shared_down(8 * n, range(FC), early_banks[n])
            choices()
            increments(range(4))
            first_tiles()
            increments(range(4, 7))
            slot_tables()
            increments(range(7, NDC))
            pe.wait_ge(tabs_ready, 4)
            pe.wait_ge(dc_read, NDC)
            pe.wait_ge(ld_e, 32 * NX)
            regs = {}

            def experts_of(v, s):
                regs["e"] = experts_window(pe, v, s)

            def expert(s, off):
                return regs["e"][8 + s % XUNROLL - off]

            def experts_pe(v, s):
                if alive(s, 4) or alive(s, 7):
                    b = (s - 4) % 2
                    if s >= 6:
                        pe.wait_ge(xa_ready, v - 5)
                    if alive(s, 4):
                        t = v - 4
                        pe.wait_ge(hx_loaded[(s - 4) % 8], (t - (s - 4) % 8) * 2 + 16)
                        for c in range(KC):
                            ins = pe.transpose(ps_x[b][:, c * P:(c + 1) * P], hx[:, (s - 4) % 8, c * P:(c + 1) * P], id_sb[:, :])
                    if alive(s, 7):
                        pe.wait_ge(act_ready, v - 6)
                        ins = pe.transpose(ps_x[b][:, E:E + F], act_x[:, (s - 7) % 4, :], id_sb[:, :])
                    ins.then_inc(xa_done, 1)
                if alive(s, 5):
                    t, b = v - 5, (s - 5) % 2
                    pe.wait_ge(xa_ready, t + 1)
                    if s - 5 >= 2:
                        pe.wait_ge(act_ready, t - 1)
                    for c in range(KC):
                        ins = pe.matmul(ps_gu[b][:, 0:2 * F], xa[:, b, c * P:(c + 1) * P],
                                        wgu_sb[:, c, bass.ds(expert(s, 5), 1), :].rearrange("p e n -> p (e n)"), start=(c == 0), stop=(c == KC - 1))
                    ins.then_inc(gu_done, 1)
                if alive(s, 8):
                    t, b = v - 8, (s - 8) % 2
                    pe.wait_ge(xa_ready, v - 4)
                    if s - 8 >= 2:
                        pe.wait_ge(y_ready, t - 1)
                    pe.matmul(ps_y[b][:, 0:E], xa[:, (s - 5) % 2, E:E + F], wd_sb[:, bass.ds(expert(s, 8), 1), :].rearrange("p e n -> p (e n)"), start=True, stop=True).then_inc(dn_done, 1)
                n8, stage = shared_now(v, s)
                if stage is not None and stage < 4:
                    shared_gate_up(n8, [stage])
                if stage in (5, 6):
                    shared_down(n8, [stage - 5])
                if alive(s, 0):
                    t = v
                    pe.wait_ge(step_ready, t + 1)
                    if s >= 1:
                        pe.wait_ge(idx_ready, t)
                    pe.matmul(ps_i[:, 0:DCW], step_sb[:, s % 2, :], dc[:, bass.ds(expert(s, 0), 1), :].rearrange("p e n -> p (e n)"), start=True, stop=True).then_inc(i_done, 1)
            run_steps(pe, XSTEPS, XHEAD, XTAIL, XUNROLL, experts_pe, experts_of)


def kernel(**inputs):
    import concourse.bacc as bacc
    from concourse.bass_utils import run_bass_kernel_spmd

    c = np.ascontiguousarray
    given = {k: np.asarray(v) for k, v in inputs.items()}
    attn = {k[8:]: v for k, v in given.items() if k.startswith("L0_attn_")}
    cond2 = {k[9:]: v for k, v in given.items() if k.startswith("L0_cond2_")}
    ffn = {k[7:]: v for k, v in given.items() if k.startswith("L0_ffn_")}

    def column(bias):
        return c(bias.reshape(KC, P).T)

    arrays = dict(
        x=c(given["x"].reshape(T, E)), subj=c(given["itok_B_0_7"].reshape(B, 1)).view(np.uint32),
        fside=c(given["fside_8xS_0"]), adapter=c(given["itok_B_0_6"]),
        wcond=c(given["L0_cond_weights"].reshape(SUBJ, S * S)),
        wq=c(attn["Wq"].T), bq=column(attn["bq"]), wk=c(attn["Wk"].T), bk=column(attn["bk"]),
        wv=c(attn["Wv"].T), bv=column(attn["bv"]), wo=c(attn["Wo"].T), bo=c(attn["bo"]),
        w2=c(cond2["W"].T), at=c(cond2["A"].reshape(P, E).T), scal=c(np.repeat(cond2["scalings"], RANK).reshape(P, 1)),
        bm=c(cond2["Bm"].transpose(0, 2, 1).reshape(P, E)), wg=c(ffn["w_gate"].T),
        wgu=c(np.concatenate([ffn["wg"], ffn["wu"]], 2).transpose(1, 0, 2)), wd=c(ffn["wd"]),
        sg=c(ffn["sg"].T), su=c(ffn["su"].T), sd=c(ffn["sd"].T), **shape_tables())

    nc = bacc.Bacc("TRN2", target_bir_lowering=False, num_devices=1)
    aps = {name: nc.dram_tensor(name, a.shape, mybir.dt.from_np(a.dtype), kind="ExternalInput").ap()
           for name, a in arrays.items()}
    aps["out"] = nc.dram_tensor("out", (T, E), F32, kind="ExternalOutput").ap()
    forward(nc, **aps)
    result = run_bass_kernel_spmd(nc, [arrays], core_ids=[0])
    return np.asarray(result.results[0]["out"]).reshape(B, S, E)


def shape_tables():
    bf16 = mybir.dt.np(BF16)
    p, e, j = np.arange(P), np.arange(NX), np.arange(SLOT_TILES)
    slopes = np.array([2.0 ** (-8.0 * (h + 1) / H) for h in range(H)], np.float32)
    query, key = p % S, np.arange(S)
    distance = np.abs(key[None, :] - query[:, None]).astype(np.float32)
    alibi = -slopes[None, :, None] * distance[:, None, :]
    alibi = np.where((key[None, :] > query[:, None])[:, None, :], np.float32(MASKED), alibi)
    tri = np.zeros((P, 2, DCW), np.float32)
    tri[:, 0, :P] = p[:, None] <= p[None, :]
    tri[:, 1, :P] = p[:, None] > p[None, :]
    tail2, tailr = np.zeros((2, NI), np.float32), np.zeros((2, DCW), np.float32)
    tail2[0, NI - 1], tail2[1, 1:] = 1, 1
    tailr[0, :P], tailr[1, P] = p + 1, P
    ecols = np.zeros((NX, 4 * NX + 2), np.float32)
    ecols[:, 0:NX] = e[:, None] < e[None, :]
    ecols[:, NX:2 * NX] = e[:, None]
    ecols[:, 2 * NX:3 * NX] = 1
    ecols[:, 3 * NX:4 * NX + 1] = -1
    ecols[NX - 1, 4 * NX + 1] = 1e6
    return dict(alibi=alibi, ident=np.eye(P, dtype=np.float32),
                headmask=(p[:, None] // D == np.arange(HC)).astype(np.float32),
                quadmask=(p[:, None] // S == np.arange(NB)).astype(np.float32),
                acol=(p // RANK).astype(np.float32).reshape(P, 1), pcol=p.astype(np.float32).reshape(P, 1),
                tri=tri.astype(bf16), tail2=tail2.astype(bf16), tailr=tailr.astype(bf16),
                iotas=np.ascontiguousarray(np.broadcast_to(np.stack([j, P * j]).astype(np.float32), (NI, 2, SLOT_TILES))),
                ecols=ecols)
```
